# Optimizing a Trainium2 kernel written in Bass

```python
import numpy as np
import jax
import jax.numpy as jnp

def _softmax(x, axis=-1):
    return jax.nn.softmax(x, axis=axis)

def _gelu(x):
    return jax.nn.gelu(x, approximate=True)

def _silu(x):
    return jax.nn.silu(x)

def _sigmoid(x):
    return jax.nn.sigmoid(x)

def _layernorm(x, axis=-1, eps=1e-05):
    m = jnp.mean(x, axis=axis, keepdims=True)
    v = jnp.var(x, axis=axis, keepdims=True)
    return (x - m) / jnp.sqrt(v + eps)

def _scatter_add(tgt, idx, src, axis=0):
    return tgt.at[idx].add(src)

def _segment_sum(src, seg, n):
    return jax.ops.segment_sum(src, seg, n)
kernel_name = 'mk_cond_seq_d4_seqx_r4_5aba22'

def setup_inputs(seed: int=0):
    np.random.seed(seed)
    _w = jnp.asarray

    def _rec_inputs():
        import jax
        import jax.numpy as jnp
        _rk = jax.random.key(seed)
        x = 7.22e-05 + 1 * jax.random.normal(jax.random.fold_in(_rk, 1), (8, 256, 256), jnp.float32)
        _lenS = 256 - jax.random.randint(jax.random.fold_in(_rk, 7), (8,), 0, max(1, 256 // 4) + 1, jnp.int32)
        _lenS2 = 256 - jax.random.randint(jax.random.fold_in(_rk, 8), (8,), 0, max(1, 256 // 4) + 1, jnp.int32)
        cond_1024 = 0.0061147 + 1.02565 * jax.random.normal(jax.random.fold_in(_rk, 11), (8, 256), jnp.float32)
        return (x, cond_1024)
    x, cond_1024 = _rec_inputs()

    def _L0_cond_setup():
        import jax, jax.numpy as jnp
        import numpy as np
        D_MODEL = 256
        NHEAD = 16
        HEAD_DIM = D_MODEL // NHEAD
        D_FF = 1024
        EPS = 1e-05

        def _layernorm(x):
            mu = jnp.mean(x, axis=-1, keepdims=True)
            var = jnp.var(x, axis=-1, keepdims=True)
            return (x - mu) * jax.lax.rsqrt(var + EPS)
        key = jax.random.key(seed)
        ks = jax.random.split(key, 16)
        B, N = (4, 512)
        s = 0.02
        inp = {'x': jax.random.normal(ks[0], (B, N, D_MODEL), jnp.float32), 'c': jax.random.normal(ks[1], (B, D_MODEL), jnp.float32), 'W_ada': jax.random.normal(ks[2], (D_MODEL, 6 * D_MODEL), jnp.float32) * s, 'b_ada': jnp.zeros((6 * D_MODEL,), jnp.float32), 'Wq': jax.random.normal(ks[3], (D_MODEL, D_MODEL), jnp.float32) * s, 'bq': jnp.zeros((D_MODEL,), jnp.float32), 'Wk': jax.random.normal(ks[4], (D_MODEL, D_MODEL), jnp.float32) * s, 'bk': jnp.zeros((D_MODEL,), jnp.float32), 'Wv': jax.random.normal(ks[5], (D_MODEL, D_MODEL), jnp.float32) * s, 'bv': jnp.zeros((D_MODEL,), jnp.float32), 'Wo': jax.random.normal(ks[6], (D_MODEL, D_MODEL), jnp.float32) * s, 'bo': jnp.zeros((D_MODEL,), jnp.float32), 'W1': jax.random.normal(ks[7], (D_MODEL, D_FF), jnp.float32) * s, 'b1': jnp.zeros((D_FF,), jnp.float32), 'W2': jax.random.normal(ks[8], (D_FF, D_MODEL), jnp.float32) * s, 'b2': jnp.zeros((D_MODEL,), jnp.float32)}
        return inp
    _L0_cond_all = _L0_cond_setup()
    _L0_cond_in = {k: v for k, v in _L0_cond_all.items() if k in ('W_ada', 'b_ada', 'Wq', 'bq', 'Wk', 'bk', 'Wv', 'bv', 'Wo', 'bo', 'W1', 'b1', 'W2', 'b2')}
    del _L0_cond_all

    def _L1_cond_setup():
        import jax, jax.numpy as jnp
        import numpy as np
        D = 256
        H = 16
        HD = 4 * D
        B, T = (4, 256)
        EPS = 1e-05

        def _layernorm(x, g, b):
            mu = jnp.mean(x, axis=-1, keepdims=True)
            var = jnp.mean(jnp.square(x - mu), axis=-1, keepdims=True)
            return (x - mu) * jax.lax.rsqrt(var + EPS) * g + b

        def _attention(x, Wqkv, Wproj, bproj):
            b, t, c = x.shape
            hd = c // H
            qkv = (x @ Wqkv).reshape(b, t, 3, H, hd).transpose(2, 0, 3, 1, 4)
            q, k, v = (qkv[0], qkv[1], qkv[2])
            scale = hd ** (-0.5)
            scores = jnp.einsum('bhqd,bhkd->bhqk', q, k) * scale
            causal = jnp.tril(jnp.ones((t, t), bool))
            scores = jnp.where(causal, scores, -jnp.inf)
            attn = jax.nn.softmax(scores, axis=-1)
            out = jnp.einsum('bhqk,bhkd->bhqd', attn, v)
            out = out.transpose(0, 2, 1, 3).reshape(b, t, c)
            return out @ Wproj + bproj
        key = jax.random.key(seed)
        ks = jax.random.split(key, 12)
        s = 0.02
        return {'x': jax.random.normal(ks[0], (B, T, D), jnp.float32), 'condition': jax.random.normal(ks[1], (B, D), jnp.float32), 'Wqkv': jax.random.normal(ks[2], (D, 3 * D), jnp.float32) * s, 'Wproj': jax.random.normal(ks[3], (D, D), jnp.float32) * s, 'bproj': jnp.zeros((D,), jnp.float32), 'W1': jax.random.normal(ks[4], (D, HD), jnp.float32) * s, 'b1': jnp.zeros((HD,), jnp.float32), 'W2': jax.random.normal(ks[5], (HD, D), jnp.float32) * s, 'b2': jnp.zeros((D,), jnp.float32), 'g1': jnp.ones((D,), jnp.float32), 'be1': jnp.zeros((D,), jnp.float32), 'g2': jnp.ones((D,), jnp.float32), 'be2': jnp.zeros((D,), jnp.float32), 'Wada': jax.random.normal(ks[6], (D, 6 * D), jnp.float32) * s, 'bada': jax.random.normal(ks[7], (6 * D,), jnp.float32) * s}
    _L1_cond_all = _L1_cond_setup()
    _L1_cond_in = {k: v for k, v in _L1_cond_all.items() if k in ('Wqkv', 'Wproj', 'bproj', 'W1', 'b1', 'W2', 'b2', 'g1', 'be1', 'g2', 'be2', 'Wada', 'bada')}
    del _L1_cond_all

    def _L2_cond_setup():
        import jax, jax.numpy as jnp
        import numpy as np
        EPS = 1e-05

        def _sln(h, w, ln_g, ln_b, Wg, bg, Wb, bb):
            mu = jnp.mean(h, axis=-1, keepdims=True)
            var = jnp.mean((h - mu) ** 2, axis=-1, keepdims=True)
            ln = (h - mu) / jnp.sqrt(var + EPS) * ln_g + ln_b
            gamma = (w @ Wg.T + bg)[:, None, :]
            beta = (w @ Wb.T + bb)[:, None, :]
            return gamma * ln + beta
        key = jax.random.key(seed)
        ks = jax.random.split(key, 20)
        B, N, D = (4, 256, 256)
        F = 4 * D
        s = lambda fan: 1.0 / np.sqrt(fan)
        inp = {'hidden': jax.random.normal(ks[0], (B, N, D), jnp.float32), 'w': jax.random.normal(ks[1], (B, D), jnp.float32), 'ln_g': jnp.ones((D,), jnp.float32), 'ln_b': jnp.zeros((D,), jnp.float32), 'Wg': jax.random.normal(ks[2], (D, D), jnp.float32) * s(D), 'bg': jnp.zeros((D,), jnp.float32), 'Wb': jax.random.normal(ks[3], (D, D), jnp.float32) * s(D), 'bb': jnp.zeros((D,), jnp.float32), 'Wqkv': jax.random.normal(ks[4], (3 * D, D), jnp.float32) * s(D), 'bqkv': jnp.zeros((3 * D,), jnp.float32), 'Wp': jax.random.normal(ks[5], (D, D), jnp.float32) * s(D), 'bp': jnp.zeros((D,), jnp.float32), 'W1': jax.random.normal(ks[6], (F, D), jnp.float32) * s(D), 'b1': jnp.zeros((F,), jnp.float32), 'W2': jax.random.normal(ks[7], (D, F), jnp.float32) * s(F), 'b2': jnp.zeros((D,), jnp.float32), 'num_heads': 16}
        return inp
    _L2_cond_all = _L2_cond_setup()
    _L2_cond_in = {k: v for k, v in _L2_cond_all.items() if k in ('ln_g', 'ln_b', 'Wg', 'bg', 'Wb', 'bb', 'Wqkv', 'bqkv', 'Wp', 'bp', 'W1', 'b1', 'W2', 'b2')}
    del _L2_cond_all

    def _L3_cond_setup():
        import jax, jax.numpy as jnp
        import numpy as np
        D = 256
        H = 16
        HD = D // H
        MLP = 4 * D

        def _lin(key, fin, fout):
            k1, k2 = jax.random.split(key)
            lim = 1.0 / np.sqrt(fin)
            W = jax.random.uniform(k1, (fin, fout), minval=-lim, maxval=lim, dtype=jnp.float32)
            b = jax.random.uniform(k2, (fout,), minval=-lim, maxval=lim, dtype=jnp.float32)
            return (W, b)

        def layernorm(x, g, b, eps=1e-05):
            mu = jnp.mean(x, axis=-1, keepdims=True)
            var = jnp.var(x, axis=-1, keepdims=True)
            return (x - mu) * jax.lax.rsqrt(var + eps) * g + b

        def attention(h, Wqkv, bqkv, Wproj, bproj):
            B, L, _ = h.shape
            qkv = (h @ Wqkv + bqkv).reshape(B, L, 3, H, HD)
            q, k, v = jnp.moveaxis(qkv, 2, 0)
            scale = HD ** (-0.5)
            attn = jnp.einsum('blhd,bmhd->bhlm', q, k) * scale
            attn = jax.nn.softmax(attn, axis=-1)
            out = jnp.einsum('bhlm,bmhd->blhd', attn, v).reshape(B, L, D)
            return out @ Wproj + bproj
        key = jax.random.key(seed)
        ks = jax.random.split(key, 10)
        x = jax.random.normal(ks[0], (4, 512, D), dtype=jnp.float32)
        time_emb = jax.random.normal(ks[1], (4, D), dtype=jnp.float32)
        Wqkv, bqkv = _lin(ks[2], D, 3 * D)
        Wproj, bproj = _lin(ks[3], D, D)
        W1, b1 = _lin(ks[4], D, MLP)
        W2, b2 = _lin(ks[5], MLP, D)
        Wt, bt = _lin(ks[6], D, 6 * D)
        g1 = jnp.ones((D,), jnp.float32)
        be1 = jnp.zeros((D,), jnp.float32)
        g2 = jnp.ones((D,), jnp.float32)
        be2 = jnp.zeros((D,), jnp.float32)
        return {'x': x, 'time_emb': time_emb, 'Wqkv': Wqkv, 'bqkv': bqkv, 'Wproj': Wproj, 'bproj': bproj, 'W1': W1, 'b1': b1, 'W2': W2, 'b2': b2, 'Wt': Wt, 'bt': bt, 'g1': g1, 'be1': be1, 'g2': g2, 'be2': be2}
    _L3_cond_all = _L3_cond_setup()
    _L3_cond_in = {k: v for k, v in _L3_cond_all.items() if k in ('Wqkv', 'bqkv', 'Wproj', 'bproj', 'W1', 'b1', 'W2', 'b2', 'Wt', 'bt', 'g1', 'be1', 'g2', 'be2')}
    del _L3_cond_all
    return {'x': x, 'cond_1024': cond_1024, 'L0_cond_W_ada': _L0_cond_in['W_ada'], 'L0_cond_b_ada': _L0_cond_in['b_ada'], 'L0_cond_Wq': _L0_cond_in['Wq'], 'L0_cond_bq': _L0_cond_in['bq'], 'L0_cond_Wk': _L0_cond_in['Wk'], 'L0_cond_bk': _L0_cond_in['bk'], 'L0_cond_Wv': _L0_cond_in['Wv'], 'L0_cond_bv': _L0_cond_in['bv'], 'L0_cond_Wo': _L0_cond_in['Wo'], 'L0_cond_bo': _L0_cond_in['bo'], 'L0_cond_W1': _L0_cond_in['W1'], 'L0_cond_b1': _L0_cond_in['b1'], 'L0_cond_W2': _L0_cond_in['W2'], 'L0_cond_b2': _L0_cond_in['b2'], 'L1_cond_Wqkv': _L1_cond_in['Wqkv'], 'L1_cond_Wproj': _L1_cond_in['Wproj'], 'L1_cond_bproj': _L1_cond_in['bproj'], 'L1_cond_W1': _L1_cond_in['W1'], 'L1_cond_b1': _L1_cond_in['b1'], 'L1_cond_W2': _L1_cond_in['W2'], 'L1_cond_b2': _L1_cond_in['b2'], 'L1_cond_g1': _L1_cond_in['g1'], 'L1_cond_be1': _L1_cond_in['be1'], 'L1_cond_g2': _L1_cond_in['g2'], 'L1_cond_be2': _L1_cond_in['be2'], 'L1_cond_Wada': _L1_cond_in['Wada'], 'L1_cond_bada': _L1_cond_in['bada'], 'L2_cond_ln_g': _L2_cond_in['ln_g'], 'L2_cond_ln_b': _L2_cond_in['ln_b'], 'L2_cond_Wg': _L2_cond_in['Wg'], 'L2_cond_bg': _L2_cond_in['bg'], 'L2_cond_Wb': _L2_cond_in['Wb'], 'L2_cond_bb': _L2_cond_in['bb'], 'L2_cond_Wqkv': _L2_cond_in['Wqkv'], 'L2_cond_bqkv': _L2_cond_in['bqkv'], 'L2_cond_Wp': _L2_cond_in['Wp'], 'L2_cond_bp': _L2_cond_in['bp'], 'L2_cond_W1': _L2_cond_in['W1'], 'L2_cond_b1': _L2_cond_in['b1'], 'L2_cond_W2': _L2_cond_in['W2'], 'L2_cond_b2': _L2_cond_in['b2'], 'L3_cond_Wqkv': _L3_cond_in['Wqkv'], 'L3_cond_bqkv': _L3_cond_in['bqkv'], 'L3_cond_Wproj': _L3_cond_in['Wproj'], 'L3_cond_bproj': _L3_cond_in['bproj'], 'L3_cond_W1': _L3_cond_in['W1'], 'L3_cond_b1': _L3_cond_in['b1'], 'L3_cond_W2': _L3_cond_in['W2'], 'L3_cond_b2': _L3_cond_in['b2'], 'L3_cond_Wt': _L3_cond_in['Wt'], 'L3_cond_bt': _L3_cond_in['bt'], 'L3_cond_g1': _L3_cond_in['g1'], 'L3_cond_be1': _L3_cond_in['be1'], 'L3_cond_g2': _L3_cond_in['g2'], 'L3_cond_be2': _L3_cond_in['be2']}

def reference(x, cond_1024, L0_cond_W_ada, L0_cond_b_ada, L0_cond_Wq, L0_cond_bq, L0_cond_Wk, L0_cond_bk, L0_cond_Wv, L0_cond_bv, L0_cond_Wo, L0_cond_bo, L0_cond_W1, L0_cond_b1, L0_cond_W2, L0_cond_b2, L1_cond_Wqkv, L1_cond_Wproj, L1_cond_bproj, L1_cond_W1, L1_cond_b1, L1_cond_W2, L1_cond_b2, L1_cond_g1, L1_cond_be1, L1_cond_g2, L1_cond_be2, L1_cond_Wada, L1_cond_bada, L2_cond_ln_g, L2_cond_ln_b, L2_cond_Wg, L2_cond_bg, L2_cond_Wb, L2_cond_bb, L2_cond_Wqkv, L2_cond_bqkv, L2_cond_Wp, L2_cond_bp, L2_cond_W1, L2_cond_b1, L2_cond_W2, L2_cond_b2, L3_cond_Wqkv, L3_cond_bqkv, L3_cond_Wproj, L3_cond_bproj, L3_cond_W1, L3_cond_b1, L3_cond_W2, L3_cond_b2, L3_cond_Wt, L3_cond_bt, L3_cond_g1, L3_cond_be1, L3_cond_g2, L3_cond_be2):
    import jax
    import jax.numpy as jnp

    def _L0_cond_ref(x, c, W_ada, b_ada, Wq, bq, Wk, bk, Wv, bv, Wo, bo, W1, b1, W2, b2):
        import jax, jax.numpy as jnp
        import numpy as np
        D_MODEL = 256
        NHEAD = 16
        HEAD_DIM = D_MODEL // NHEAD
        D_FF = 1024
        EPS = 1e-05

        def _layernorm(x):
            mu = jnp.mean(x, axis=-1, keepdims=True)
            var = jnp.var(x, axis=-1, keepdims=True)
            return (x - mu) * jax.lax.rsqrt(var + EPS)
        B, N, _ = x.shape
        ada = (c @ W_ada + b_ada)[:, None, :]
        shift1, scale1, gate1, shift2, scale2, gate2 = jnp.split(ada, 6, axis=-1)
        h = _layernorm(x) * (1.0 + scale1) + shift1
        Q = (h @ Wq + bq).reshape(B, N, NHEAD, HEAD_DIM)
        K = (h @ Wk + bk).reshape(B, N, NHEAD, HEAD_DIM)
        V = (h @ Wv + bv).reshape(B, N, NHEAD, HEAD_DIM)
        scores = jnp.einsum('bqhd,bkhd->bhqk', Q, K) / np.sqrt(HEAD_DIM).astype(np.float32)
        attn = jax.nn.softmax(scores, axis=-1)
        attn_out = jnp.einsum('bhqk,bkhd->bqhd', attn, V).reshape(B, N, D_MODEL)
        attn_out = attn_out @ Wo + bo
        x = x + gate1 * attn_out
        h = _layernorm(x) * (1.0 + scale2) + shift2
        ff = jax.nn.gelu(h @ W1 + b1, approximate=False) @ W2 + b2
        return x + gate2 * ff

    def _L1_cond_ref(x, condition, Wqkv, Wproj, bproj, W1, b1, W2, b2, g1, be1, g2, be2, Wada, bada):
        import jax, jax.numpy as jnp
        import numpy as np
        D = 256
        H = 16
        HD = 4 * D
        B, T = (4, 256)
        EPS = 1e-05

        def _layernorm(x, g, b):
            mu = jnp.mean(x, axis=-1, keepdims=True)
            var = jnp.mean(jnp.square(x - mu), axis=-1, keepdims=True)
            return (x - mu) * jax.lax.rsqrt(var + EPS) * g + b

        def _attention(x, Wqkv, Wproj, bproj):
            b, t, c = x.shape
            hd = c // H
            qkv = (x @ Wqkv).reshape(b, t, 3, H, hd).transpose(2, 0, 3, 1, 4)
            q, k, v = (qkv[0], qkv[1], qkv[2])
            scale = hd ** (-0.5)
            scores = jnp.einsum('bhqd,bhkd->bhqk', q, k) * scale
            causal = jnp.tril(jnp.ones((t, t), bool))
            scores = jnp.where(causal, scores, -jnp.inf)
            attn = jax.nn.softmax(scores, axis=-1)
            out = jnp.einsum('bhqk,bhkd->bhqd', attn, v)
            out = out.transpose(0, 2, 1, 3).reshape(b, t, c)
            return out @ Wproj + bproj
        mod = jax.nn.silu(condition) @ Wada + bada
        sh_a, sc_a, gt_a, sh_m, sc_m, gt_m = jnp.split(mod, 6, axis=1)
        xn = _layernorm(x, g1, be1)
        xm = xn * (1.0 + sc_a[:, None, :]) + sh_a[:, None, :]
        x = x + gt_a[:, None, :] * _attention(xm, Wqkv, Wproj, bproj)
        xn = _layernorm(x, g2, be2)
        xm = xn * (1.0 + sc_m[:, None, :]) + sh_m[:, None, :]
        h = jax.nn.gelu(xm @ W1 + b1, approximate=False)
        x = x + gt_m[:, None, :] * (h @ W2 + b2)
        return x

    def _L2_cond_ref(hidden, w, ln_g, ln_b, Wg, bg, Wb, bb, Wqkv, bqkv, Wp, bp, W1, b1, W2, b2, num_heads):
        import jax, jax.numpy as jnp
        import numpy as np
        EPS = 1e-05

        def _sln(h, w, ln_g, ln_b, Wg, bg, Wb, bb):
            mu = jnp.mean(h, axis=-1, keepdims=True)
            var = jnp.mean((h - mu) ** 2, axis=-1, keepdims=True)
            ln = (h - mu) / jnp.sqrt(var + EPS) * ln_g + ln_b
            gamma = (w @ Wg.T + bg)[:, None, :]
            beta = (w @ Wb.T + bb)[:, None, :]
            return gamma * ln + beta
        B, N, D = hidden.shape
        hd = D // num_heads
        h = _sln(hidden, w, ln_g, ln_b, Wg, bg, Wb, bb)
        qkv = (h @ Wqkv.T + bqkv).reshape(B, N, num_heads, hd, 3)
        q = jnp.moveaxis(qkv[..., 0], 2, 1)
        k = jnp.moveaxis(qkv[..., 1], 2, 1)
        v = jnp.moveaxis(qkv[..., 2], 2, 1)
        energy = jnp.einsum('bhqd,bhkd->bhqk', q, k)
        att = jax.nn.softmax(energy, axis=-1) / D ** 0.5
        out = jnp.einsum('bhqk,bhkd->bhqd', att, v)
        out = jnp.moveaxis(out, 1, 2).reshape(B, N, D)
        out = out @ Wp.T + bp
        h1 = out + hidden
        h2 = _sln(h1, w, ln_g, ln_b, Wg, bg, Wb, bb)
        return h2 + h1

    def _L3_cond_ref(x, time_emb, Wqkv, bqkv, Wproj, bproj, W1, b1, W2, b2, Wt, bt, g1, be1, g2, be2):
        import jax, jax.numpy as jnp
        import numpy as np
        D = 256
        H = 16
        HD = D // H
        MLP = 4 * D

        def _lin(key, fin, fout):
            k1, k2 = jax.random.split(key)
            lim = 1.0 / np.sqrt(fin)
            W = jax.random.uniform(k1, (fin, fout), minval=-lim, maxval=lim, dtype=jnp.float32)
            b = jax.random.uniform(k2, (fout,), minval=-lim, maxval=lim, dtype=jnp.float32)
            return (W, b)

        def layernorm(x, g, b, eps=1e-05):
            mu = jnp.mean(x, axis=-1, keepdims=True)
            var = jnp.var(x, axis=-1, keepdims=True)
            return (x - mu) * jax.lax.rsqrt(var + eps) * g + b

        def attention(h, Wqkv, bqkv, Wproj, bproj):
            B, L, _ = h.shape
            qkv = (h @ Wqkv + bqkv).reshape(B, L, 3, H, HD)
            q, k, v = jnp.moveaxis(qkv, 2, 0)
            scale = HD ** (-0.5)
            attn = jnp.einsum('blhd,bmhd->bhlm', q, k) * scale
            attn = jax.nn.softmax(attn, axis=-1)
            out = jnp.einsum('bhlm,bmhd->blhd', attn, v).reshape(B, L, D)
            return out @ Wproj + bproj
        tp = (jax.nn.silu(time_emb) @ Wt + bt)[:, None, :]
        shift_msa, scale_msa, gate_msa, shift_mlp, scale_mlp, gate_mlp = jnp.split(tp, 6, axis=-1)
        h = layernorm(x, g1, be1)
        h = h * (1.0 + scale_msa) + shift_msa
        h = attention(h, Wqkv, bqkv, Wproj, bproj)
        x = x + gate_msa * h
        h = layernorm(x, g2, be2)
        h = h * (1.0 + scale_mlp) + shift_mlp
        h = jax.nn.gelu(h @ W1 + b1, approximate=False) @ W2 + b2
        x = x + gate_mlp * h
        return x
    x = _L0_cond_ref(x, cond_1024, L0_cond_W_ada, L0_cond_b_ada, L0_cond_Wq, L0_cond_bq, L0_cond_Wk, L0_cond_bk, L0_cond_Wv, L0_cond_bv, L0_cond_Wo, L0_cond_bo, L0_cond_W1, L0_cond_b1, L0_cond_W2, L0_cond_b2)
    x = _L1_cond_ref(x, cond_1024, L1_cond_Wqkv, L1_cond_Wproj, L1_cond_bproj, L1_cond_W1, L1_cond_b1, L1_cond_W2, L1_cond_b2, L1_cond_g1, L1_cond_be1, L1_cond_g2, L1_cond_be2, L1_cond_Wada, L1_cond_bada)
    x = _L2_cond_ref(x, cond_1024, L2_cond_ln_g, L2_cond_ln_b, L2_cond_Wg, L2_cond_bg, L2_cond_Wb, L2_cond_bb, L2_cond_Wqkv, L2_cond_bqkv, L2_cond_Wp, L2_cond_bp, L2_cond_W1, L2_cond_b1, L2_cond_W2, L2_cond_b2, 16)
    x = _L3_cond_ref(x, cond_1024, L3_cond_Wqkv, L3_cond_bqkv, L3_cond_Wproj, L3_cond_bproj, L3_cond_W1, L3_cond_b1, L3_cond_W2, L3_cond_b2, L3_cond_Wt, L3_cond_bt, L3_cond_g1, L3_cond_be1, L3_cond_g2, L3_cond_be2)
    return x

_drawn_inputs = setup_inputs


def setup_inputs(seed=0):
    import zlib

    import numpy as np

    out = dict(_drawn_inputs(seed))
    spreads = {'L0_cond_b_ada': (0.0, 0.452),
     'L0_cond_bq': (0.0, 0.8),
     'L0_cond_bk': (0.0, 2.0),
     'L0_cond_bv': (0.0, 0.8),
     'L0_cond_bo': (0.0, 0.275),
     'L0_cond_b1': (0.0, 0.794),
     'L0_cond_b2': (0.0, 0.337),
     'L1_cond_bproj': (0.0, 0.515),
     'L1_cond_b1': (0.0, 0.8),
     'L1_cond_b2': (0.0, 0.522),
     'L1_cond_g1': (1.0, 0.6),
     'L1_cond_be1': (0.0, 0.8),
     'L1_cond_g2': (1.0, 0.6),
     'L1_cond_be2': (0.0, 0.8),
     'L2_cond_ln_g': (1.0, 0.2),
     'L2_cond_ln_b': (0.0, 0.272),
     'L2_cond_bg': (0.0, 0.288),
     'L2_cond_bb': (0.0, 0.28),
     'L2_cond_bqkv': (0.0, 2.0),
     'L2_cond_bp': (0.0, 0.282),
     'L2_cond_b1': (0.0, 0.1),
     'L2_cond_b2': (0.0, 0.1),
     'L3_cond_g1': (1.0, 0.6),
     'L3_cond_be1': (0.0, 0.8),
     'L3_cond_g2': (1.0, 0.6),
     'L3_cond_be2': (0.0, 2.0)}
    factors = {'L0_cond_Wq': 8.0,
     'L0_cond_Wk': 8.0,
     'L0_cond_Wv': 5.339,
     'L0_cond_Wo': 4.222,
     'L1_cond_Wqkv': 8.0,
     'L1_cond_Wproj': 8.0,
     'L1_cond_W1': 2.917,
     'L1_cond_W2': 2.692,
     'L1_cond_bada': 8.0,
     'L3_cond_bqkv': 8.0,
     'L3_cond_bproj': 8.0,
     'L3_cond_b1': 35.238,
     'L3_cond_b2': 26.52,
     'L3_cond_bt': 7.334}
    for name, (base, spread) in spreads.items():
        noise = np.random.default_rng([zlib.crc32(name.encode()), seed]).standard_normal(out[name].shape)
        drawn = base * np.exp(spread * noise) if base else spread * noise
        out[name] = jnp.asarray(drawn.astype(out[name].dtype))
    for name, factor in factors.items():
        out[name] = (out[name] * factor).astype(out[name].dtype)
    return out
```

```python
from contextlib import ExitStack

import numpy as np

import concourse.bass as bass
from concourse import mybir

P = 128
B, N, D, H, FF = 8, 256, 256, 16, 1024
HD = D // H
T = N // P
KT = D // P
FT = FF // P
PAIRS = H // 2
GROUPS = 4
LAYERS = 4
STEPS = LAYERS * B
HAS_MLP = (True, True, False, True)
CAUSAL = (False, True, False, False)
QKV_BIAS = (True, False, True, True)
SCORE_SCALE = (HD ** -0.5, HD ** -0.5, 1.0, HD ** -0.5)
EPS = 1e-5
MASKED = -1e30
KB = 3 * 2 * HD
KM = KB + 2

F32 = mybir.dt.float32
F32R = mybir.dt.float32r
BF16 = mybir.dt.bfloat16
ALU = mybir.AluOpType
ACT = mybir.ActivationFunctionType
AX = mybir.AxisListType

VECS = {}
for _l, _names in enumerate((
    (("ada", 12), ("bq", 2), ("bk", 2), ("bv", 2), ("b1", 8)),
    (("ada", 12), ("g1", 2), ("be1", 2), ("g2", 2), ("be2", 2), ("b1", 8)),
    (("lg", 2), ("lb", 2), ("bg", 2), ("bb", 2), ("bq", 2), ("bk", 2), ("bv", 2)),
    (("ada", 12), ("g1", 2), ("be1", 2), ("g2", 2), ("be2", 2), ("bq", 2), ("bk", 2), ("bv", 2), ("b1", 8)),
)):
    for _n, _c in _names:
        VECS[_l, _n] = (sum(c for _, c in VECS.values()), _c)
NVEC = sum(c for _, c in VECS.values())

O_QKV, O_O = 0, KT * 3 * D
O_1 = O_O + KT * D
O_2 = O_1 + KT * FF
WCOLS = O_2 + FT * D
ADA = 6 * D
NROW = 5
NPAR = 4


class Step:

    def __init__(self, off, reg=None):
        self.off, self.reg = off, reg
        self.layer, self.par = off // B, off % 2

    def back(self, n):
        return Step(self.off - n, self.reg)

    def ahead(self, n):
        return Step(self.off + n, self.reg)

    @property
    def exists(self):
        return self.reg is not None or 0 <= self.off < STEPS

    @property
    def seq(self):
        b = self.off % B
        return b if self.reg is None else self.reg + b

    def _value(self, first, per, c):
        value = first * per + c
        if self.reg is None:
            return value
        assert value > 0
        return self.reg * per + value

    def count(self, per, c):
        return self._value(self.off, per, c)

    def mlp(self, per, c):
        return self._value(self.off - (B if self.layer > 2 else 0), per, c)


def cond_seq_blocks(nc, x, cond_t, vecs, rows, ada, weights, out):
    par_dram = nc.dram_tensor("par_dram", (LAYERS, B, NPAR, D), F32).ap()
    qk_dram = nc.dram_tensor("qk_dram", (2, 4, 2 * HD, PAIRS, N), F32).ap()

    with ExitStack() as ctx:
        def sb(name, shape, dt=F32):
            return ctx.enter_context(nc.sbuf_tensor(name, shape, dt))

        def sem(name):
            return ctx.enter_context(nc.semaphore(name))

        x_sb = sb("x_sb", [P, B, T, D])
        w_sb = [sb(f"w_sb{i}", [P, WCOLS]) for i in range(2)]
        ada_sb = sb("ada_sb", [P, KT, ADA])
        vec = sb("vec", [P, NVEC])
        cond_sb = sb("cond_sb", [P, KT, B])
        silu_sb = sb("silu_sb", [P, KT, B])
        silu_t = sb("silu_t", [P, KT, B])
        mod = sb("mod", [P, LAYERS, 2, 2, KT, B])
        mod_t = sb("mod_t", [P, KT, B])
        row_in = sb("row_in", [B, NROW, D])
        row_out = sb("row_out", [B, NPAR, D])
        row_t = sb("row_t", [B, 2, D])
        par_sb = [sb(f"par_sb{i}", [P, NPAR, D]) for i in range(2)]
        q_stack = [sb(f"q_stack{i}", [P, H, N]) for i in range(2)]
        k_stack = [sb(f"k_stack{i}", [P, PAIRS, N]) for i in range(2)]
        v_aug = [sb(f"v_aug{i}", [P, T, H, 2 * HD]) for i in range(2)]
        xn1 = sb("xn1", [P, T, D])
        xn2 = sb("xn2", [P, T, D])
        ht1 = sb("ht1", [P, KT, N])
        ht2 = sb("ht2", [P, KT, N])
        q_hi, q_lo, k_hi, k_lo = (sb(n, [P, KT, N]) for n in ("q_hi", "q_lo", "k_hi", "k_lo"))
        neg_max = sb("neg_max", [P, T, H])
        max_parts = sb("max_parts", [P, 2, T, 2, H // 2])
        max_t = [sb(f"max_t{i}", [H, N]) for i in range(2)]
        probs = [sb(f"probs{i}", [P, T, 2, N]) for i in range(4)]
        o_sb = [sb(f"o_sb{i}", [P, N]) for i in range(2)]
        rec = sb("rec", [P, T, 4])
        bv_scaled = sb("bv_scaled", [P, KT])
        ao = sb("ao", [P, T, D])
        ao_t = sb("ao_t", [P, KT, N])
        hid = sb("hid", [P, FT, N])
        xg = sb("xg", [P, T, D])
        prod = sb("prod", [P, T, D])
        stats = sb("stats", [P, 2, T, 6])
        mv = sb("mv", [P, 2, T, 2])
        veps = sb("veps", [P, 2, T])
        rstd = sb("rstd", [P, 2, T])
        eps_c = sb("eps_c", [P, T])
        half_c = sb("half_c", [P, T])
        ident = sb("ident", [P, P])
        ident_b = sb("ident_b", [P, P], BF16)
        mask_q = sb("mask_q", [P, 2, P], BF16)
        mask_k = sb("mask_k", [P, 2, P], BF16)

        dense = [ctx.enter_context(nc.psum_tensor(f"dense{i}", [P, 512], F32)) for i in range(2)]
        s_bank = [ctx.enter_context(nc.psum_tensor(f"s_bank{i}", [P, 512], F32)) for i in range(2)]
        st_bank = [ctx.enter_context(nc.psum_tensor(f"st_bank{i}", [P, 512], F32)) for i in range(2)]
        o_bank = [ctx.enter_context(nc.psum_tensor(f"o_bank{i}", [P, 512], F32)) for i in range(2)]

        cond_ld, vec_ld, row_ld, ada_ld, w_ld = (sem(n) for n in ("cond_ld", "vec_ld", "row_ld", "ada_ld", "w_ld"))
        w_ld = [w_ld, sem("w_ld1"), sem("w_ld2"), sem("w_ld3")]
        x_ld = [sem(f"x_ld{i}") for i in range(3)]
        consts, cleared, stacks_filled = sem("consts"), sem("cleared"), sem("stacks_filled")
        silu_exp, silu_chain, silu_done = sem("silu_exp"), sem("silu_chain"), sem("silu_done")
        mod_ps, mod_chain, mod_done, par_st = sem("mod_ps"), sem("mod_chain"), sem("mod_done"), sem("par_st")
        par_ld = sem("par_ld")
        ln1_stats, ln1_mv, ln1_veps, ln1_rstd, xn1_done = (
            sem(n) for n in ("ln1_stats", "ln1_mv", "ln1_veps", "ln1_rstd", "xn1_done"))
        ln2_stats, ln2_mv, ln2_veps, ln2_rstd, xn2_done = (
            sem(n) for n in ("ln2_stats", "ln2_mv", "ln2_veps", "ln2_rstd", "xn2_done"))
        ht1_ps, ht1_sb, q_ps, k_ps, v_ps = (sem(n) for n in ("ht1_ps", "ht1_sb", "q_ps", "k_ps", "v_ps"))
        q_hi_sb, q_lo_sb, k_hi_sb, k_lo_sb, v_sb = (
            sem(n) for n in ("q_hi_sb", "q_lo_sb", "k_hi_sb", "k_lo_sb", "v_sb"))
        qk_spill, stack_ld = sem("qk_spill"), sem("stack_ld")
        s_ps, s_max, max_hi, max_lo, max_ps, max_sb, max_ld = (
            sem(n) for n in ("s_ps", "s_max", "max_hi", "max_lo", "max_ps", "max_sb", "max_ld"))
        st_ps, p_sb, o_ps, o_copy, ot_ps, rec_sb, ao_sb = (
            sem(n) for n in ("st_ps", "p_sb", "o_ps", "o_copy", "ot_ps", "rec_sb", "ao_sb"))
        aot_ps, aot_sb, proj_ps, prod1, xg1, x1_done = (
            sem(n) for n in ("aot_ps", "aot_sb", "proj_ps", "prod1", "xg1", "x1_done"))
        ht2_ps, ht2_sb, w1_ps, gelu_sb, w2_ps, prod2, xg2, x2_done = (
            sem(n) for n in ("ht2_ps", "ht2_sb", "w1_ps", "gelu_sb", "w2_ps", "prod2", "xg2", "x2_done"))
        out_st = sem("out_st")

        def col(l, name, i):
            c = VECS[l, name][0] + i
            return vec[:, c:c + 1]

        def w_qkv(l, kt, c0, c1):
            return w_sb[l % 2][:, O_QKV + kt * 3 * D + c0:O_QKV + kt * 3 * D + c1]

        def w_o(l, kt):
            return w_sb[l % 2][:, O_O + kt * D:O_O + (kt + 1) * D]

        def w_1(l, kt, j):
            return w_sb[l % 2][:, O_1 + kt * FF + j * P:O_1 + kt * FF + (j + 1) * P]

        def w_2(l, j):
            return w_sb[l % 2][:, O_2 + j * D:O_2 + (j + 1) * D]

        def wait(eng, s, value):
            if not isinstance(value, int) or value > 0:
                eng.wait_ge(s, value)

        def run_steps(eng, step, boundary):
            for l in range(LAYERS):
                step(Step(l * B))
                boundary(l)
                first = 1 if 0 < l < LAYERS - 1 else 3
                for b in range(1, first):
                    step(Step(l * B + b))
                with eng.Fori(0, B - 1 - first, 2) as r:
                    r = nc.s_assert_within(r, 0, B - 3 - first, skip_runtime_bounds_check_because="the loop's last value")
                    step(Step(l * B + first, r))
                    step(Step(l * B + first + 1, r))
                step(Step(l * B + B - 1))

        def split3(ap):
            return ap.rearrange("p (a n) -> p a n", a=2)

        block = ctx.enter_context(nc.Block())

        @block.sync
        def _(sp):
            sp.dma_start(cond_sb[:], cond_t).then_inc(cond_ld, 16)
            sp.dma_start(vec[:], vecs).then_inc(vec_ld, 16)
            sp.dma_start(x_sb[:, 0], x[0].rearrange("(t p) d -> p t d", p=P)).then_inc(x_ld[0], 16)
            sp.dma_start(ada_sb[:], ada[0]).then_inc(ada_ld, 16)
            sp.dma_start(row_in[:], rows[0].partition_broadcast(B)).then_inc(row_ld, 16)
            sp.dma_start(w_sb[0][:], weights[0]).then_inc(w_ld[0], 16)
            sp.dma_start(x_sb[:, 1], x[1].rearrange("(t p) d -> p t d", p=P)).then_inc(x_ld[1], 16)
            for t in range(T):
                sp.dma_start(x_sb[:, 2:B, t], x[2:B].rearrange("b (t p) d -> t p b d", p=P)[t]).then_inc(x_ld[2], 16)

            def store_rows(l):
                sp.wait_ge(mod_done, l + 1)
                sp.dma_start(par_dram[l], row_out[:]).then_inc(par_st, 16)

            def next_modulation(l):
                if l < LAYERS:
                    sp.wait_ge(mod_done, l)
                    n = 1 if l == 2 else 3
                    sp.dma_start(ada_sb[:, :, 0:n * 2 * D], ada[l]).then_inc(ada_ld, 16)
                    sp.dma_start(row_in[:], rows[l].partition_broadcast(B)).then_inc(row_ld, 16)

            def spill_and_stack(a):
                for part, tile, ready in ((0, q_hi, q_hi_sb), (1, q_lo, q_lo_sb), (2, k_hi, k_hi_sb), (3, k_lo, k_lo_sb)):
                    wait(sp, ready, a.count(1, 1))
                    dst = qk_dram[a.par, part].rearrange("r (t j) n -> j r t n", j=4)
                    sp.dma_start(dst, tile[:]).then_inc(qk_spill, 16)
                wait(sp, qk_spill, a.count(64, 64))
                for quad, part in enumerate((0, 0, 1)):
                    for e in range(2):
                        r0 = quad * 2 * HD + e * HD
                        src = qk_dram[a.par, part, e * HD:(e + 1) * HD]
                        dst = q_stack[a.par][r0:r0 + HD].rearrange("r (p e) n -> r p e n", e=2)[:, :, e, :]
                        sp.dma_start(dst, src).then_inc(stack_ld, 16)
                for quad, part in enumerate((2, 3, 2)):
                    r0 = quad * 2 * HD
                    sp.dma_start(k_stack[a.par][r0:r0 + 2 * HD], qk_dram[a.par, part]).then_inc(stack_ld, 16)

            def max_rows(g, half):
                wait(sp, max_sb, g.count(2, half + 1))
                h0 = half * H // 2
                for part in range(2):
                    dst = q_stack[g.par][KB + part:KB + part + 1, h0:h0 + H // 2, :]
                    src = max_t[half][part * H // 2:(part + 1) * H // 2, :]
                    sp.dma_start(dst, src).then_inc(max_ld, 16)

            def step(g):
                a, done = g.ahead(1), g.back(2)
                max_rows(g, 0)
                sp.wait_ge(par_st, 16 * (g.layer + 1))
                src = par_dram[g.layer].rearrange("b r d -> b (r d)")[bass.ds(g.seq, 1) if g.reg is not None else slice(g.seq, g.seq + 1)]
                sp.dma_start(par_sb[g.par][:].rearrange("p r d -> p (r d)"),
                             src.rearrange("b n -> (b n)").partition_broadcast(P)).then_inc(par_ld, 16)
                if done.exists and done.layer == LAYERS - 1:
                    store(done)
                if a.exists:
                    spill_and_stack(a)
                max_rows(g, 1)

            def store(c):
                b = c.seq
                if c.reg is None:
                    sp.dma_start(out[b].rearrange("(t p) d -> p t d", p=P), x_sb[:, b]).then_inc(out_st, 16)
                else:
                    dst = out[bass.ds(b, 1)].rearrange("b (t p) d -> p (b t) d", p=P)
                    sp.dma_start(dst, x_sb[:, bass.ds(b, 1)].rearrange("p b t d -> p (b t) d")).then_inc(out_st, 16)

            def boundary(l):
                if l + 1 < LAYERS:
                    wait(sp, x2_done, Step(l * B - 1).count(1, 1))
                    wait(sp, proj_ps, Step(l * B - 1).count(1, 1))
                    sp.wait_ge(mod_done, l + 1)
                    n = O_1 if l + 1 == 2 else WCOLS
                    sp.dma_start(w_sb[(l + 1) % 2][:, 0:n], weights[l + 1]).then_inc(w_ld[l + 1], 16)
                    store_rows(l + 1)
                    next_modulation(l + 2)

            store_rows(0)
            next_modulation(1)
            sp.wait_ge(stacks_filled, 6)
            spill_and_stack(Step(0))
            run_steps(sp, step, boundary)
            for i in (Step(STEPS - 2), Step(STEPS - 1)):
                sp.wait_ge(x2_done, i.count(1, 1))
                store(i)
            sp.wait_ge(out_st, 16 * B)

        @block.gpsimd
        def _(pool):
            nc.gpsimd.memset(ident[:], 0.0).then_inc(cleared, 1)
            nc.gpsimd.memset(ident_b[:], 0.0).then_inc(cleared, 1)
            nc.gpsimd.memset(mask_q[:], 0.0).then_inc(cleared, 1)
            nc.gpsimd.memset(mask_k[:], 0.0).then_inc(cleared, 1)
            nc.gpsimd.memset(eps_c[:], EPS).then_inc(consts, 1)
            nc.gpsimd.memset(half_c[:], -0.5).then_inc(consts, 1)
            pool.wait_ge(cleared, 4)
            for m in (ident, ident_b):
                nc.gpsimd.affine_select(out=m[:], in_=m[:], compare_op=ALU.not_equal, fill=1.0, base=0,
                                        pattern=[[-1, P]], channel_multiplier=1).then_inc(consts, 1)
            nc.gpsimd.affine_select(out=mask_q[:], in_=mask_q[:], compare_op=ALU.is_ge, fill=MASKED, base=0,
                                    pattern=[[0, 2], [-1, P]], channel_multiplier=1).then_inc(consts, 1)
            nc.gpsimd.affine_select(out=mask_k[:], in_=mask_k[:], compare_op=ALU.is_ge, fill=MASKED, base=0,
                                    pattern=[[0, 2], [1, P]], channel_multiplier=-1).then_inc(consts, 1)
            pool.wait_ge(consts, 2)

            def power(i, which, mv_s, veps_s, rstd_s):
                wait(pool, mv_s, i.count(1, 1))
                nc.gpsimd.tensor_tensor(veps[:, which, :], mv[:, which, :, 1], eps_c[:], ALU.add).then_inc(veps_s, 1)
                wait(pool, veps_s, i.count(1, 1))
                nc.gpsimd.tensor_tensor(rstd[:, which, :], veps[:, which, :], half_c[:], ALU.pow).then_inc(rstd_s, 1)

            def addend(c, row, s):
                sl = x_sb[:, bass.ds(c.seq, 1)] if c.reg is not None else x_sb[:, c.seq:c.seq + 1]
                for t in range(T):
                    ins = nc.gpsimd.tensor_tensor(xg[:, t:t + 1, :], sl[:, 0, t:t + 1], par_sb[c.par][:, row:row + 1, :], ALU.add)
                ins.then_inc(s, 1)

            def step(g):
                c, a = g.back(1), g.ahead(1)
                if c.exists:
                    wait(pool, x2_done, c.count(1, 0))
                    wait(pool, par_ld, c.count(16, 16))
                if a.exists:
                    power(a, 0, ln1_mv, ln1_veps, ln1_rstd)
                if c.exists:
                    addends(c)

            def addends(c):
                addend(c, 1, xg1)
                power(c, 1, ln2_mv, ln2_veps, ln2_rstd)
                addend(c, 3, xg2)

            power(Step(0), 0, ln1_mv, ln1_veps, ln1_rstd)
            run_steps(pool, step, lambda l: None)
            step_last = Step(STEPS - 1)
            wait(pool, x2_done, step_last.count(1, 0))
            wait(pool, par_ld, step_last.count(16, 16))
            addends(step_last)

        @block.scalar
        def _(act):
            act.wait_ge(cond_ld, 16)
            nc.scalar.activation(silu_t[:], cond_sb[:], ACT.Exp, scale=-1.0).then_inc(silu_exp, 1)

            def hi_parts(a):
                l = a.layer
                for which, ps, bank, dst, done, spilled in (
                        ("bq", q_ps, 0, q_hi, q_hi_sb, qk_spill), ("bk", k_ps, 1, k_hi, k_hi_sb, qk_spill)):
                    wait(act, spilled, a.count(64, 0))
                    wait(act, ps, a.count(1, 1))
                    src = split3(dense[bank][:])
                    if QKV_BIAS[l]:
                        for t in range(KT):
                            ins = nc.scalar.activation(dst[:, t].bitcast(F32R), src[:, t], ACT.Identity,
                                                       bias=col(l, which, t))
                    else:
                        ins = nc.scalar.activation(dst[:].bitcast(F32R), src, ACT.Identity)
                    ins.then_inc(done, 1)
                wait(act, v_ps, a.count(1, 1))
                wait(act, o_ps, a.count(4, 4 - 2 * 4))
                if a.off < 2:
                    act.wait_ge(stacks_filled, 6)
                src = dense[0][:].rearrange("p (t h d) -> p t h d", t=T, h=H)
                nc.scalar.activation(v_aug[a.par][:, :, :, 0:HD], src, ACT.Copy).then_inc(v_sb, 1)

            def ao_transposed(c):
                l = c.layer
                wait(act, aot_ps, c.count(1, 1))
                wait(act, proj_ps, c.count(1, 0))
                src = split3(dense[1][:])
                for t in range(KT):
                    dst = ao_t[:, t]
                    if l == 1:
                        ins = nc.scalar.activation(dst, src[:, t], ACT.Identity)
                    elif l == 2:
                        ins = nc.scalar.activation(dst, src[:, t], ACT.Identity, scale=D ** -0.5, bias=bv_scaled[:, t:t + 1])
                    else:
                        ins = nc.scalar.activation(dst, src[:, t], ACT.Identity, bias=col(l, "bv", t))
                ins.then_inc(aot_sb, 1)

            def gelus(c):
                l = c.layer
                wait(act, w2_ps, c.mlp(1, 0))
                for i in range(FT // 2):
                    wait(act, w1_ps, c.mlp(4, i + 1))
                    src = split3(dense[i % 2][:])
                    for k in range(2):
                        ins = nc.scalar.activation(hid[:, 2 * i + k], src[:, k], ACT.Gelu, bias=col(l, "b1", 2 * i + k))
                    ins.then_inc(gelu_sb, 1)

            def exps(g):
                l = g.layer
                for p in range(PAIRS):
                    if p % 2 == 0:
                        wait(act, o_ps, g.count(4, p // 2 - 1) if p >= 4 else g.count(4, p // 2 + 3 - 4))
                    for kt in range(T):
                        wait(act, st_ps, g.count(16, 2 * p + kt + 1))
                        q0 = P if CAUSAL[l] and kt else 0
                        src = split3(st_bank[kt][:])[:, :, q0:N]
                        nc.scalar.activation(probs[p % 4][:, kt, :, q0:N], src, ACT.Exp,
                                             scale=SCORE_SCALE[l]).then_inc(p_sb, 1)

            def step(g):
                c, a = g.back(1), g.ahead(1)
                if c.exists:
                    ao_transposed(c)
                if a.exists:
                    hi_parts(a)
                if c.exists and HAS_MLP[c.layer]:
                    gelus(c)
                exps(g)

            act.wait_ge(vec_ld, 16)
            nc.scalar.activation(bv_scaled[:], vec[:, VECS[2, "bv"][0]:VECS[2, "bv"][0] + KT], ACT.Copy,
                                 scale=D ** -0.5).then_inc(silu_exp, 1)
            act.wait_ge(silu_exp, 2)
            hi_parts(Step(0))
            run_steps(act, step, lambda l: None)
            ao_transposed(Step(STEPS - 1))
            gelus(Step(STEPS - 1))

        @block.vector
        def _(dve):
            for s in range(2):
                nc.vector.memset(q_stack[s][:], 0.0).then_inc(stacks_filled, 1)
                nc.vector.memset(k_stack[s][:], 1.0).then_inc(stacks_filled, 1)
                nc.vector.memset(v_aug[s][:], 1.0).then_inc(stacks_filled, 1)

            dve.wait_ge(silu_exp, 1)
            nc.vector.tensor_scalar(silu_t[:], silu_t[:], 1.0, None, ALU.add).then_inc(silu_chain, 1)
            dve.wait_ge(silu_chain, 1)
            nc.vector.reciprocal(silu_t[:], silu_t[:]).then_inc(silu_chain, 1)
            dve.wait_ge(silu_chain, 2)
            nc.vector.tensor_tensor(silu_sb[:], cond_sb[:], silu_t[:], ALU.mult).then_inc(silu_done, 1)

            chained = [0]

            def link(ins):
                chained[0] += 1
                ins.then_inc(mod_chain, 1)
                dve.wait_ge(mod_chain, chained[0])

            def modulation(l):
                dve.wait_ge(vec_ld, 16)
                dve.wait_ge(row_ld, 16 * (l + 1))
                dve.wait_ge(mod_ps, 2 * l + 1)
                if l > 0:
                    dve.wait_ge(par_st, 16 * l)
                cols = dense[1][:, 0:64].rearrange("p (c b) -> p c b", b=B)
                if l == 2:
                    for t in range(KT):
                        gam, bet = cols[:, t], cols[:, KT + t]
                        link(nc.vector.tensor_scalar(mod_t[:, t], gam, col(l, "bg", t), None, ALU.add))
                        nc.vector.tensor_scalar(mod[:, l, 0, 0, t], mod_t[:, t], col(l, "lg", t), None, ALU.mult)
                        link(nc.vector.tensor_scalar(mod_t[:, t], mod_t[:, t], col(l, "lb", t), None, ALU.mult))
                        link(nc.vector.scalar_tensor_tensor(mod[:, l, 0, 1, t], bet, col(l, "bb", t), mod_t[:, t],
                                                            ALU.add, ALU.add))
                else:
                    for ln in range(2):
                        for t in range(KT):
                            i = 4 * ln + t
                            v0 = 6 * ln + t
                            shift, scale = cols[:, i], cols[:, i + KT]
                            fac, add = mod[:, l, ln, 0, t], mod[:, l, ln, 1, t]
                            link(nc.vector.tensor_scalar(fac, scale, col(l, "ada", v0 + KT), 1.0, ALU.add, ALU.add))
                            if l == 0:
                                link(nc.vector.tensor_scalar(add, shift, col(l, "ada", v0), None, ALU.add))
                            else:
                                g_, be_ = col(l, f"g{ln + 1}", t), col(l, f"be{ln + 1}", t)
                                link(nc.vector.tensor_scalar(mod_t[:, t], fac, be_, col(l, "ada", v0), ALU.mult, ALU.add))
                                link(nc.vector.tensor_tensor(add, shift, mod_t[:, t], ALU.add))
                                link(nc.vector.tensor_scalar(fac, fac, g_, None, ALU.mult))
                dve.wait_ge(mod_ps, 2 * l + 2)
                r = dense[0][0:B, :].rearrange("p (a d) -> p a d", a=2)
                if l == 2:
                    link(nc.vector.tensor_tensor(row_t[:, 0], r[:, 0], row_in[:, 0], ALU.add))
                    nc.vector.tensor_tensor(row_out[:, 2], row_t[:, 0], row_in[:, 1], ALU.mult)
                    nc.vector.tensor_copy(row_out[:, 0], row_in[:, 4])
                    nc.vector.tensor_copy(row_out[:, 1], row_in[:, 4])
                    link(nc.vector.tensor_tensor(row_t[:, 1], r[:, 1], row_in[:, 2], ALU.add))
                    link(nc.vector.tensor_tensor(row_t[:, 0], row_t[:, 0], row_in[:, 3], ALU.mult))
                    nc.vector.tensor_tensor(row_out[:, 3], row_t[:, 0], row_t[:, 1], ALU.add).then_inc(mod_done, 1)
                else:
                    link(nc.vector.tensor_tensor(row_out[:, 0], r[:, 0], row_in[:, 0], ALU.add))
                    link(nc.vector.tensor_tensor(row_out[:, 2], r[:, 1], row_in[:, 2], ALU.add))
                    nc.vector.tensor_tensor(row_out[:, 1], row_out[:, 0], row_in[:, 1], ALU.mult)
                    nc.vector.tensor_tensor(row_out[:, 3], row_out[:, 2], row_in[:, 3], ALU.mult).then_inc(mod_done, 1)
                dve.wait_ge(mod_done, l + 1)

            def x_of(i):
                return x_sb[:, bass.ds(i.seq, 1)][:, 0] if i.reg is not None else x_sb[:, i.seq]

            def norm_stats(i, which, s):
                for t in range(T):
                    ins = nc.vector.bn_stats(stats[:, which, t], x_of(i)[:, t])
                ins.then_inc(s, 1)

            def norm_mv(which, s):
                for t in range(T):
                    ins = nc.vector.bn_aggr(mv[:, which, t], stats[:, which, t])
                ins.then_inc(s, 1)

            def normalize(i, which, rstd_s, dst, s):
                wait(dve, rstd_s, i.count(1, 1))
                for t in range(T):
                    ins = nc.vector.tensor_scalar(dst[:, t], x_of(i)[:, t], mv[:, which, t, 0:1], rstd[:, which, t:t + 1],
                                                  ALU.subtract, ALU.mult)
                ins.then_inc(s, 1)

            def ln1_a(i):
                if i.layer == 0:
                    for q in range(3):
                        if i.reg is not None or q <= min(i.off, 2):
                            dve.wait_ge(x_ld[q], 32 if q == 2 else 16)
                norm_stats(i, 0, ln1_stats)

            def ln1_c(i):
                wait(dve, ht1_ps, i.count(1, 0))
                normalize(i, 0, ln1_rstd, xn1, xn1_done)

            def score_max(g, j):
                p, qt = j // 2, j % 2
                wait(dve, s_ps, g.count(16, j + 1))
                bank = s_bank[(j + (j >= 8)) % 2]
                k1 = P if CAUSAL[g.layer] and qt == 0 else N
                nc.vector.tensor_reduce(neg_max[:, qt, 2 * p:2 * p + 2], split3(bank[:])[:, :, 0:k1], AX.X, ALU.max,
                                        negate=True).then_inc(s_max, 1)

            def max_split(g, half):
                h0 = half * H // 2
                hi = max_parts[:, half, :, 0]
                lo = max_parts[:, half, :, 1]
                src = neg_max[:, :, h0:h0 + H // 2]
                wait(dve, max_ps, g.count(2, half + 1 - 2))
                wait(dve, s_max, g.count(16, 8 * half + 8))
                nc.vector.tensor_copy(hi.bitcast(F32R), src).then_inc(max_hi, 1)
                wait(dve, max_hi, g.count(2, half + 1))
                nc.vector.tensor_tensor(lo.bitcast(F32R), src, hi, ALU.subtract).then_inc(max_lo, 1)

            def max_copy(g, half):
                wait(dve, max_ps, g.count(2, half + 1))
                wait(dve, max_ld, g.count(64, 32 * half + 32 - 64))
                nc.vector.tensor_copy(max_t[half][:], s_bank[half % 2][0:H, 0:N]).then_inc(max_sb, 1)

            def modulate(i, ln, bank, ps, dst, s, v):
                wait(dve, ps, v)
                src = split3(dense[bank][:])
                for t in range(KT):
                    m = mod[:, i.layer, ln]
                    if i.reg is None:
                        fac, add = m[:, 0, t, i.seq:i.seq + 1], m[:, 1, t, i.seq:i.seq + 1]
                    else:
                        fac, add = m[:, 0, t, bass.ds(i.seq, 1)], m[:, 1, t, bass.ds(i.seq, 1)]
                    ins = nc.vector.tensor_scalar(dst[:, t], src[:, t], fac, add, ALU.mult, ALU.add)
                ins.then_inc(s, 1)

            def lo_part(a, which, bank, ready, hi, dst, s):
                l = a.layer
                wait(dve, qk_spill, a.count(64, 0))
                wait(dve, ready, a.count(1, 1))
                src = split3(dense[bank][:])
                if QKV_BIAS[l]:
                    for t in range(KT):
                        ins = nc.vector.scalar_tensor_tensor(dst[:, t].bitcast(F32R), src[:, t], col(l, which, t), hi[:, t],
                                                             ALU.add, ALU.subtract)
                else:
                    ins = nc.vector.tensor_tensor(dst[:].bitcast(F32R), src, hi[:], ALU.subtract)
                ins.then_inc(s, 1)

            def times_gate(c, src, row, s):
                for t in range(T):
                    ins = nc.vector.tensor_tensor(prod[:, t], src[:, t], par_sb[c.par][:, row], ALU.mult)
                ins.then_inc(s, 1)

            def residual(c, src, s_xg, s):
                wait(dve, s_xg, c.count(1, 1))
                nc.vector.tensor_tensor(x_of(c), src, xg[:], ALU.add).then_inc(s, 1)

            def first_residual(c):
                wait(dve, proj_ps, c.count(1, 1))
                wait(dve, par_ld, c.count(16, 16))
                if c.layer == 2:
                    residual(c, split3(dense[1][:]), xg1, x1_done)
                else:
                    times_gate(c, split3(dense[1][:]), 0, prod1)
                    wait(dve, prod1, c.mlp(1, 1))
                    residual(c, prod[:], xg1, x1_done)

            def second_residual(c):
                if c.layer == 2:
                    wait(dve, xn2_done, c.count(1, 1))
                    times_gate(c, xn2, 2, prod2)
                else:
                    wait(dve, w2_ps, c.mlp(1, 1))
                    times_gate(c, split3(dense[0][:]), 2, prod2)
                wait(dve, prod2, c.count(1, 1))
                residual(c, prod[:], xg2, x2_done)

            def out_copy(g, q):
                wait(dve, o_ps, g.count(4, q + 1))
                wait(dve, ot_ps, g.count(4, q + 1 - 2))
                nc.vector.tensor_copy(o_sb[q % 2][:], o_bank[q % 2][:, 0:N]).then_inc(o_copy, 1)

            def out_norm(g, q):
                wait(dve, ot_ps, g.count(4, q + 1))
                o4 = o_bank[q % 2][:, N:2 * N].rearrange("p (t h d) -> p t h d", t=T, h=4)
                wait(dve, ao_sb, g.count(4, q))
                nc.vector.reciprocal(rec[:], o4[:, :, :, HD]).then_inc(rec_sb, 1)
                wait(dve, rec_sb, g.count(4, q + 1))
                if q == 0:
                    wait(dve, aot_ps, g.count(1, 0))
                dst = ao[:, :, 4 * HD * q:4 * HD * (q + 1)].rearrange("p t (h d) -> p t h d", h=4)
                nc.vector.tensor_tensor(dst, o4[:, :, :, 0:HD],
                                        rec[:].unsqueeze(3).to_broadcast([P, T, 4, HD]), ALU.mult).then_inc(ao_sb, 1)

            def step(g):
                c, a = g.back(1), g.ahead(1)
                mlp = c.exists and HAS_MLP[c.layer]
                if a.exists and a.layer > 0:
                    wait(dve, x2_done, a.count(1, 1 - B))
                score_max(g, 0)
                if a.exists:
                    ln1_a(a)
                    wait(dve, ln1_stats, a.count(1, 1))
                score_max(g, 1)
                if a.exists:
                    norm_mv(0, ln1_mv)
                score_max(g, 2)
                if a.exists:
                    ln1_c(a)
                score_max(g, 3)
                if c.exists:
                    first_residual(c)
                    wait(dve, x1_done, c.count(1, 1))
                score_max(g, 4)
                if a.exists:
                    wait(dve, v_ps, a.count(1, 0))
                    modulate(a, 0, 0, ht1_ps, ht1, ht1_sb, a.count(1, 1))
                if c.exists:
                    norm_stats(c, 1, ln2_stats)
                    wait(dve, ln2_stats, c.count(1, 1))
                score_max(g, 5)
                if c.exists:
                    norm_mv(1, ln2_mv)
                score_max(g, 6)
                score_max(g, 7)
                max_split(g, 0)
                if c.exists:
                    if mlp:
                        wait(dve, ht2_ps, c.mlp(1, 0))
                    normalize(c, 1, ln2_rstd, xn2, xn2_done)
                score_max(g, 8)
                max_copy(g, 0)
                if a.exists:
                    lo_part(a, "bq", 0, q_hi_sb, q_hi, q_lo, q_lo_sb)
                score_max(g, 9)
                if a.exists:
                    lo_part(a, "bk", 1, k_hi_sb, k_hi, k_lo, k_lo_sb)
                score_max(g, 10)
                score_max(g, 11)
                if mlp:
                    wait(dve, w1_ps, c.mlp(4, 0))
                    modulate(c, 1, 1, ht2_ps, ht2, ht2_sb, c.mlp(1, 1))
                for j in range(12, 16):
                    score_max(g, j)
                max_split(g, 1)
                max_copy(g, 1)
                out_copy(g, 0)
                if c.exists:
                    second_residual(c)
                out_norm(g, 0)
                out_copy(g, 1)
                out_norm(g, 1)
                out_copy(g, 2)
                out_norm(g, 2)
                out_copy(g, 3)
                out_norm(g, 3)

            def boundary(l):
                if l + 1 < LAYERS:
                    modulation(l + 1)

            first = Step(0)
            ln1_a(first)
            dve.wait_ge(ln1_stats, 1)
            norm_mv(0, ln1_mv)
            ln1_c(first)
            modulation(0)
            modulate(first, 0, 0, ht1_ps, ht1, ht1_sb, 1)
            lo_part(first, "bq", 0, q_hi_sb, q_hi, q_lo, q_lo_sb)
            lo_part(first, "bk", 1, k_hi_sb, k_hi, k_lo, k_lo_sb)
            run_steps(dve, step, boundary)
            last = Step(STEPS - 1)
            first_residual(last)
            wait(dve, x1_done, last.count(1, 1))
            norm_stats(last, 1, ln2_stats)
            dve.wait_ge(ln2_stats, last.count(1, 1))
            norm_mv(1, ln2_mv)
            normalize(last, 1, ln2_rstd, xn2, xn2_done)
            modulate(last, 1, 1, ht2_ps, ht2, ht2_sb, last.mlp(1, 1))
            second_residual(last)

        @block.tensor
        def _(pe):
            mm, tr = nc.tensor.matmul, nc.tensor.transpose

            def modulation(l):
                pe.wait_ge(ada_ld, 16 * (l + 1))
                pe.wait_ge(cond_ld, 16)
                pe.wait_ge(silu_done, 1)
                cs = silu_sb if l in (1, 3) else cond_sb
                chunks = [k * 2 + t for k in ((0, 1) if l == 2 else (0, 1, 3, 4)) for t in range(KT)]
                for i, ch in enumerate(chunks):
                    for kt in range(KT):
                        ins = mm(dense[1][:, i * B:(i + 1) * B], ada_cols(l, kt, ch * P, (ch + 1) * P), cs[:, kt],
                                 start=kt == 0, stop=kt == KT - 1)
                ins.then_inc(mod_ps, 1)
                for i, ch in enumerate((0, 1) if l == 2 else (2, 5)):
                    for kt in range(KT):
                        ins = mm(dense[0][0:B, i * D:(i + 1) * D], cs[:, kt], ada_cols(l, kt, ch * D, (ch + 1) * D),
                                 start=kt == 0, stop=kt == KT - 1)
                ins.then_inc(mod_ps, 1)

            def ada_cols(l, kt, c0, c1):
                return ada_sb[:, kt, c0:c1]

            def transposed(bank, src, ready):
                for t in range(T):
                    for kt in range(KT):
                        ins = tr(bank[:, kt * N + t * P:kt * N + (t + 1) * P], src[:, t, kt * P:(kt + 1) * P], ident[:])
                ins.then_inc(ready, 1)

            def ht1_t(a):
                wait(pe, xn1_done, a.count(1, 1))
                c = a.back(2)
                wait(pe, v_sb, a.count(1, 0))
                if c.off > 0 or c.reg is not None:
                    wait(pe, prod2, c.count(1, 0))
                transposed(dense[0], xn1, ht1_ps)

            def q_product(a):
                pe.wait_ge(w_ld[a.layer], 16)
                wait(pe, ht1_sb, a.count(1, 1))
                qk_product(a, 0, 0, q_ps)

            def qk_product(a, which, bank, ready):
                for t in range(KT):
                    for kt in range(KT):
                        c0 = which * D + t * P
                        ins = mm(dense[bank][:, t * N:(t + 1) * N], w_qkv(a.layer, kt, c0, c0 + P), ht1[:, kt],
                                 start=kt == 0, stop=kt == KT - 1)
                ins.then_inc(ready, 1)

            def k_product(a):
                c = a.back(2)
                if c.exists and c.off >= 0:
                    wait(pe, x1_done, c.count(1, 1))
                qk_product(a, 1, 1, k_ps)

            def v_product(a):
                wait(pe, q_lo_sb, a.count(1, 1))
                for t in range(T):
                    for kt in range(KT):
                        ins = mm(dense[0][:, t * D:(t + 1) * D], ht1[:, kt, t * P:(t + 1) * P],
                                 w_qkv(a.layer, kt, 2 * D, 3 * D), start=kt == 0, stop=kt == KT - 1)
                ins.then_inc(v_ps, 1)

            def ao_t_t(c):
                wait(pe, ao_sb, c.count(4, 4))
                wait(pe, k_lo_sb, c.count(1, 2) if c.off + 1 < STEPS else c.count(1, 1))
                transposed(dense[1], ao, aot_ps)

            def projection(c):
                wait(pe, aot_sb, c.count(1, 1))
                for t in range(T):
                    for kt in range(KT):
                        ins = mm(dense[1][:, t * D:(t + 1) * D], ao_t[:, kt, t * P:(t + 1) * P], w_o(c.layer, kt),
                                 start=kt == 0, stop=kt == KT - 1)
                ins.then_inc(proj_ps, 1)

            def ht2_t(c, a):
                wait(pe, xn2_done, c.count(1, 1))
                if a is not None and a.exists:
                    wait(pe, k_lo_sb, a.count(1, 1))
                wait(pe, x1_done, c.count(1, 1))
                transposed(dense[1], xn2, ht2_ps)

            def mlp_up(c, a, i):
                if i == 0:
                    wait(pe, ht2_sb, c.mlp(1, 1))
                    if a is not None and a.exists:
                        wait(pe, v_sb, a.count(1, 1))
                elif i >= 2:
                    wait(pe, gelu_sb, c.mlp(4, i - 1))
                for k in range(2):
                    for kt in range(KT):
                        ins = mm(dense[i % 2][:, k * N:(k + 1) * N], w_1(c.layer, kt, 2 * i + k), ht2[:, kt],
                                 start=kt == 0, stop=kt == KT - 1)
                ins.then_inc(w1_ps, 1)

            def mlp_down(c, t):
                if t == 0:
                    wait(pe, gelu_sb, c.mlp(4, 4))
                for j in range(FT):
                    ins = mm(dense[0][:, t * D:(t + 1) * D], hid[:, j, t * P:(t + 1) * P], w_2(c.layer, j),
                             start=j == 0, stop=j == FT - 1)
                if t == T - 1:
                    ins.then_inc(w2_ps, 1)

            def score(g, *tiles):
                for j in tiles:
                    p, qt = j // 2, j % 2
                    pos = j + (j >= 8)
                    if j == 0:
                        wait(pe, stack_ld, g.count(144, 144))
                        wait(pe, s_max, g.count(16, 0))
                    elif j == 1:
                        wait(pe, max_sb, g.count(2, 0))
                    elif j == 9:
                        wait(pe, max_sb, g.count(2, 1))
                    elif j == 8:
                        wait(pe, s_max, g.count(16, 8))
                    else:
                        wait(pe, s_max, g.count(16, j - 1))
                    bank = s_bank[pos % 2]
                    causal = CAUSAL[g.layer]
                    k1 = P if causal and qt == 0 else N
                    for e in range(2):
                        ins = mm(bank[:, e * N:e * N + k1],
                                 q_stack[g.par][0:KB, 2 * p + e, qt * P:(qt + 1) * P].bitcast(F32R),
                                 k_stack[g.par][0:KB, p, 0:k1].bitcast(F32R), start=True, stop=not causal)
                        if causal:
                            ins = mm(bank[:, e * N + k1 - P:e * N + k1], ident_b[:], mask_q[:, 0], start=False, stop=True)
                    ins.then_inc(s_ps, 1)

            def max_turn(g, half):
                wait(pe, max_lo, g.count(2, half + 1))
                wait(pe, s_max, g.count(16, 7 if half == 0 else 16))
                for qt in range(T):
                    ins = tr(s_bank[half % 2][0:H, qt * P:(qt + 1) * P],
                             max_parts[:, half, qt].rearrange("p a h -> p (a h)"), ident[:])
                ins.then_inc(max_ps, 1)

            def score_t(g, *pairs):
                for p in pairs:
                    if p == 0:
                        wait(pe, max_ld, g.count(64, 32))
                    if p == PAIRS // 2:
                        wait(pe, max_ld, g.count(64, 64))
                    for kt in range(T):
                        wait(pe, p_sb, g.count(16, 2 * p + kt - 1))
                        causal = CAUSAL[g.layer]
                        q0 = P if causal and kt else 0
                        bank = split3(st_bank[kt][:])
                        ins = mm(bank[:, :, q0:N], k_stack[g.par][0:KM, p, kt * P:(kt + 1) * P].bitcast(F32R),
                                 q_stack[g.par][0:KM, 2 * p:2 * p + 2, q0:N].bitcast(F32R), start=True, stop=not causal)
                        if causal:
                            ins = mm(bank[:, :, kt * P:(kt + 1) * P], ident_b[:], mask_k[:], start=False, stop=True)
                        ins.then_inc(st_ps, 1)

            def values(g, q):
                wait(pe, v_sb, g.count(1, 1))
                wait(pe, ao_sb, g.count(4, q - 1))
                wait(pe, p_sb, g.count(16, 4 * q + 4))
                for kt in range(T):
                    q0 = P if CAUSAL[g.layer] and kt else 0
                    for j in range(4):
                        pr = probs[(2 * q + j // 2) % 4]
                        ins = mm(o_bank[q % 2][32 * j:32 * j + 32, q0:N], v_aug[g.par][:, kt, 4 * q + j, :],
                                 pr[:, kt, j % 2, q0:N], start=kt == 0, stop=kt == T - 1)
                ins.then_inc(o_ps, 1)

            def out_turn(g, q):
                wait(pe, o_copy, g.count(4, q + 1))
                for t in range(T):
                    ins = tr(o_bank[q % 2][:, N + t * P:N + (t + 1) * P], o_sb[q % 2][:, t * P:(t + 1) * P], ident[:])
                ins.then_inc(ot_ps, 1)

            def step(g):
                c, a = g.back(1), g.ahead(1)
                mlp = c.exists and HAS_MLP[c.layer]
                if c.exists:
                    ao_t_t(c)
                score(g, 0, 1, 2)
                if c.exists:
                    projection(c)
                score(g, 3)
                if a.exists:
                    ht1_t(a)
                score(g, 4, 5, 6)
                if a.exists:
                    q_product(a)
                score(g, 7)
                if a.exists:
                    k_product(a)
                max_turn(g, 0)
                score(g, 8, 9)
                if a.exists:
                    v_product(a)
                score(g, 10, 11)
                if mlp:
                    ht2_t(c, a)
                score(g, 12)
                if mlp:
                    mlp_up(c, a, 0)
                score(g, 13)
                if mlp:
                    mlp_up(c, a, 1)
                score(g, 14, 15)
                if mlp:
                    mlp_up(c, a, 2)
                score_t(g, 0)
                if mlp:
                    mlp_up(c, a, 3)
                max_turn(g, 1)
                score_t(g, 1)
                if mlp:
                    mlp_down(c, 0)
                score_t(g, 2)
                values(g, 0)
                if mlp:
                    mlp_down(c, 1)
                score_t(g, 3)
                out_turn(g, 0)
                score_t(g, 4)
                values(g, 1)
                score_t(g, 5)
                out_turn(g, 1)
                score_t(g, 6)
                values(g, 2)
                score_t(g, 7)
                out_turn(g, 2)
                values(g, 3)
                out_turn(g, 3)

            def boundary(l):
                if l + 1 < LAYERS:
                    wait(pe, prod2, Step(l * B - 1).count(1, 1))
                    pe.wait_ge(v_sb, l * B + 2)
                    pe.wait_ge(k_lo_sb, l * B + 2)
                    if l and HAS_MLP[l - 1]:
                        pe.wait_ge(gelu_sb, Step(l * B - 1).mlp(4, 4))
                    modulation(l + 1)
                    pe.wait_ge(mod_done, l + 2)

            pe.wait_ge(consts, 6)
            modulation(0)
            pe.wait_ge(mod_done, 1)
            first = Step(0)
            ht1_t(first)
            q_product(first)
            k_product(first)
            v_product(first)
            run_steps(pe, step, boundary)
            last = Step(STEPS - 1)
            ao_t_t(last)
            projection(last)
            ht2_t(last, None)
            for i in range(FT // 2):
                mlp_up(last, None, i)
            for t in range(T):
                mlp_down(last, t)


def _pack(inputs):
    g = {k: np.asarray(v) for k, v in inputs.items()}

    def tiles(w):
        return w.reshape(-1, P, w.shape[1]).transpose(1, 0, 2)

    def L(l, name):
        return g[f"L{l}_cond_{name}"]

    qkv2 = L(2, "Wqkv").reshape(D, 3, D).transpose(2, 1, 0).reshape(D, 3 * D)
    bqkv2 = L(2, "bqkv").reshape(D, 3).T
    weights = [
        (np.concatenate([L(0, "Wq"), L(0, "Wk"), L(0, "Wv")], 1), L(0, "Wo"), L(0, "W1"), L(0, "W2")),
        (L(1, "Wqkv"), L(1, "Wproj"), L(1, "W1"), L(1, "W2")),
        (qkv2, L(2, "Wp").T),
        (L(3, "Wqkv"), L(3, "Wproj"), L(3, "W1"), L(3, "W2")),
    ]
    ada = [L(0, "W_ada"), L(1, "Wada"), np.concatenate([L(2, "Wg").T, L(2, "Wb").T], 1), L(3, "Wt")]
    biases = (L(0, "b_ada"), L(1, "bada"), None, L(3, "bt"))
    vec = {
        (0, "ada"): biases[0], (0, "bq"): L(0, "bq"), (0, "bk"): L(0, "bk"), (0, "bv"): L(0, "bv"), (0, "b1"): L(0, "b1"),
        (1, "ada"): biases[1], (1, "b1"): L(1, "b1"),
        (2, "lg"): L(2, "ln_g"), (2, "lb"): L(2, "ln_b"), (2, "bg"): L(2, "bg"), (2, "bb"): L(2, "bb"),
        (2, "bq"): bqkv2[0], (2, "bk"): bqkv2[1], (2, "bv"): bqkv2[2],
        (3, "ada"): biases[3], (3, "bq"): L(3, "bqkv")[0:D], (3, "bk"): L(3, "bqkv")[D:2 * D],
        (3, "bv"): L(3, "bqkv")[2 * D:], (3, "b1"): L(3, "b1"),
    }
    for l in (1, 3):
        for n in ("g1", "be1", "g2", "be2"):
            vec[l, n] = L(l, n)
    vecs = np.concatenate([vec[k].reshape(-1, P) for k in VECS], 0).T
    rows = []
    for l in range(LAYERS):
        if l == 2:
            r = [L(2, "bg"), L(2, "ln_g"), L(2, "bb"), L(2, "ln_b"), L(2, "bp")]
        else:
            bo, b2 = L(l, "bo" if l == 0 else "bproj"), L(l, "b2")
            r = [biases[l][2 * D:3 * D], bo, biases[l][5 * D:], b2, b2]
        rows.append(np.stack(r))
    packed = {"x": g["x"], "cond_t": g["cond_1024"].T.reshape(KT, P, B).transpose(1, 0, 2), "vecs": vecs,
              "rows": np.stack(rows)}
    for l in range(LAYERS):
        packed[f"ada{l}"] = tiles(ada[l])
        packed[f"w{l}"] = np.concatenate([tiles(w).reshape(P, -1) for w in weights[l]], 1)
    return {k: np.ascontiguousarray(v) for k, v in packed.items()}


def kernel(**inputs):
    import concourse.bacc as _bacc
    from concourse.bass_utils import run_bass_kernel_spmd as _run

    nc = _bacc.Bacc("TRN2", target_bir_lowering=False, num_devices=1)
    arrays = _pack(inputs)
    t = {k: nc.dram_tensor(k, a.shape, mybir.dt.from_np(a.dtype), kind="ExternalInput").ap() for k, a in arrays.items()}
    out = nc.dram_tensor("out", (B, N, D), F32, kind="ExternalOutput").ap()
    cond_seq_blocks(nc, t["x"], t["cond_t"], t["vecs"], t["rows"], [t[f"ada{l}"] for l in range(LAYERS)],
                    [t[f"w{l}"] for l in range(LAYERS)], out)
    return _run(nc, [arrays], core_ids=[0]).results[0]["out"]
```

```python
from contextlib import ExitStack

import numpy as np

import concourse.bass as bass
from concourse import mybir

P = 128
B, N, D, H, FF = 8, 256, 256, 16, 1024
HD = D // H
T = N // P
KT = D // P
FT = FF // P
PAIRS = H // 2
GROUPS = 4
LAYERS = 4
STEPS = LAYERS * B
HAS_MLP = (True, True, False, True)
CAUSAL = (False, True, False, False)
QKV_BIAS = (True, False, True, True)
SCORE_SCALE = (HD ** -0.5, HD ** -0.5, 1.0, HD ** -0.5)
EPS = 1e-5
MASKED = -1e30
KB = 3 * 2 * HD
KM = KB + 2

F32 = mybir.dt.float32
F32R = mybir.dt.float32r
BF16 = mybir.dt.bfloat16
ALU = mybir.AluOpType
ACT = mybir.ActivationFunctionType
AX = mybir.AxisListType

VECS = {}
for _l, _names in enumerate((
    (("ada", 12), ("bq", 2), ("bk", 2), ("bv", 2), ("b1", 8)),
    (("ada", 12), ("g1", 2), ("be1", 2), ("g2", 2), ("be2", 2), ("b1", 8)),
    (("lg", 2), ("lb", 2), ("bg", 2), ("bb", 2), ("bq", 2), ("bk", 2), ("bv", 2)),
    (("ada", 12), ("g1", 2), ("be1", 2), ("g2", 2), ("be2", 2), ("bq", 2), ("bk", 2), ("bv", 2), ("b1", 8)),
)):
    for _n, _c in _names:
        VECS[_l, _n] = (sum(c for _, c in VECS.values()), _c)
NVEC = sum(c for _, c in VECS.values())

O_QKV, O_O = 0, KT * 3 * D
O_1 = O_O + KT * D
O_2 = O_1 + KT * FF
WCOLS = O_2 + FT * D
ADA = 6 * D
NROW = 5
NPAR = 4


class Step:

    def __init__(self, off, reg=None):
        self.off, self.reg = off, reg
        self.layer, self.par = off // B, off % 2

    def back(self, n):
        return Step(self.off - n, self.reg)

    def ahead(self, n):
        return Step(self.off + n, self.reg)

    @property
    def exists(self):
        return self.reg is not None or 0 <= self.off < STEPS

    @property
    def seq(self):
        b = self.off % B
        return b if self.reg is None else self.reg + b

    @property
    def wrapped_seq(self):
        return self.seq if self.reg is None else (self.reg + self.off % B) % B

    def _value(self, first, per, c):
        value = first * per + c
        if self.reg is None:
            return value
        assert value > 0
        return self.reg * per + value

    def count(self, per, c):
        return self._value(self.off, per, c)

    def mlp(self, per, c):
        return self._value(self.off - (B if self.layer > 2 else 0), per, c)


def cond_seq_blocks(nc, x, cond_t, vecs, rows, ada, weights, out):
    par_dram = nc.dram_tensor("par_dram", (LAYERS, B, NPAR, D), F32).ap()
    qk_dram = nc.dram_tensor("qk_dram", (2, 4, 2 * HD, PAIRS, N), F32).ap()

    with ExitStack() as ctx:
        def sb(name, shape, dt=F32):
            return ctx.enter_context(nc.sbuf_tensor(name, shape, dt))

        def sem(name):
            return ctx.enter_context(nc.semaphore(name))

        x_sb = sb("x_sb", [P, B, T, D])
        w_sb = [sb(f"w_sb{i}", [P, WCOLS]) for i in range(2)]
        ada_sb = sb("ada_sb", [P, KT, ADA])
        vec = sb("vec", [P, NVEC])
        cond_sb = sb("cond_sb", [P, KT, B])
        silu_sb = sb("silu_sb", [P, KT, B])
        silu_t = sb("silu_t", [P, KT, B])
        mod = sb("mod", [P, LAYERS, 2, 2, KT, B])
        mod_now = sb("mod_now", [P, 2, 2, KT, 1])
        mod_t = sb("mod_t", [P, KT, B])
        row_in = sb("row_in", [B, NROW, D])
        row_out = sb("row_out", [B, NPAR, D])
        par_sb = [sb(f"par_sb{i}", [P, NPAR, D]) for i in range(2)]
        q_stack = [sb(f"q_stack{i}", [P, H, N]) for i in range(2)]
        k_stack = [sb(f"k_stack{i}", [P, PAIRS, N]) for i in range(2)]
        v_aug = [sb(f"v_aug{i}", [P, T, H, 2 * HD]) for i in range(2)]
        xn1 = sb("xn1", [P, T, D])
        xn2 = sb("xn2", [P, T, D])
        ht1 = sb("ht1", [P, KT, N])
        ht2 = sb("ht2", [P, KT, N])
        q_hi, q_lo, k_hi, k_lo = (sb(n, [P, KT, N]) for n in ("q_hi", "q_lo", "k_hi", "k_lo"))
        neg_max = sb("neg_max", [P, T, H])
        max_parts = sb("max_parts", [P, 2, T, 2, H // 2])
        max_t = [sb(f"max_t{i}", [H, N]) for i in range(2)]
        probs = [sb(f"probs{i}", [P, T, 2, N]) for i in range(4)]
        o_sb = [sb(f"o_sb{i}", [P, N]) for i in range(2)]
        rec = sb("rec", [P, T, 4])
        bv_scaled = sb("bv_scaled", [P, KT])
        ao = sb("ao", [P, T, D])
        ao_t = sb("ao_t", [P, KT, N])
        hid = sb("hid", [P, FT, N])
        xg = [sb(f"xg{i}", [P, T, D]) for i in range(2)]
        x1 = xg[0]
        prod = sb("prod", [P, T, D])
        row_t = prod[0:B]
        stats = sb("stats", [P, 2, T, 6])
        mv = sb("mv", [P, 2, T, 2])
        veps = sb("veps", [P, 2, T])
        rstd = sb("rstd", [P, 2, T])
        eps_c = sb("eps_c", [P, T])
        half_c = sb("half_c", [P, T])
        ident = sb("ident", [P, P])
        ident_b = sb("ident_b", [P, P], BF16)
        mask_q = sb("mask_q", [P, 2, P], BF16)
        mask_k = sb("mask_k", [P, 2, P], BF16)

        dense = [ctx.enter_context(nc.psum_tensor(f"dense{i}", [P, 512], F32)) for i in range(2)]
        s_bank = [ctx.enter_context(nc.psum_tensor(f"s_bank{i}", [P, 512], F32)) for i in range(2)]
        st_bank = [ctx.enter_context(nc.psum_tensor(f"st_bank{i}", [P, 512], F32)) for i in range(2)]
        o_bank = [ctx.enter_context(nc.psum_tensor(f"o_bank{i}", [P, 512], F32)) for i in range(2)]

        cond_ld, vec_ld, row_ld, ada_ld = (sem(n) for n in ("cond_ld", "vec_ld", "row_ld", "ada_ld"))
        wqkv_ld = [sem(f"wqkv_ld{l}") for l in range(LAYERS)]
        w_ld = [sem(f"w_ld{l}") for l in range(LAYERS)]
        x_ld = [sem(f"x_ld{i}") for i in range(3)]
        consts, cleared, q_filled, kv_filled = sem("consts"), sem("cleared"), sem("q_filled"), sem("kv_filled")
        mod_cols = sem("mod_cols")
        silu_exp, silu_chain, silu_done = sem("silu_exp"), sem("silu_chain"), sem("silu_done")
        mod_ps, mod_chain, mod_done, par_st = sem("mod_ps"), sem("mod_chain"), sem("mod_done"), sem("par_st")
        par_ld = sem("par_ld")
        ln1_stats, ln1_mv, ln1_veps, ln1_rstd, xn1_done = (
            sem(n) for n in ("ln1_stats", "ln1_mv", "ln1_veps", "ln1_rstd", "xn1_done"))
        ln2_stats, ln2_mv, ln2_veps, ln2_rstd, xn2_done = (
            sem(n) for n in ("ln2_stats", "ln2_mv", "ln2_veps", "ln2_rstd", "xn2_done"))
        ht1_ps, ht1_sb, q_ps, k_ps, v_ps = (sem(n) for n in ("ht1_ps", "ht1_sb", "q_ps", "k_ps", "v_ps"))
        q_hi_sb, q_lo_sb, k_hi_sb, k_lo_sb, v_sb = (
            sem(n) for n in ("q_hi_sb", "q_lo_sb", "k_hi_sb", "k_lo_sb", "v_sb"))
        qk_spill, stack_ld = sem("qk_spill"), sem("stack_ld")
        s_ps, s_max, max_hi, max_lo, max_ps, max_sb, max_ld = (
            sem(n) for n in ("s_ps", "s_max", "max_hi", "max_lo", "max_ps", "max_sb", "max_ld"))
        st_ps, p_sb, o_ps, o_copy, ot_ps, rec_sb, ao_sb = (
            sem(n) for n in ("st_ps", "p_sb", "o_ps", "o_copy", "ot_ps", "rec_sb", "ao_sb"))
        aot_ps, aot_sb, proj_ps, prod1, xg1, x1_done = (
            sem(n) for n in ("aot_ps", "aot_sb", "proj_ps", "prod1", "xg1", "x1_done"))
        mod1_now, mod2_now = sem("mod1_now"), sem("mod2_now")
        ht2_ps, ht2_sb, w1_ps, gelu_sb, w2_ps, prod2, xg2, x2_done = (
            sem(n) for n in ("ht2_ps", "ht2_sb", "w1_ps", "gelu_sb", "w2_ps", "prod2", "xg2", "x2_done"))
        out_st = sem("out_st")

        def col(l, name, i):
            c = VECS[l, name][0] + i
            return vec[:, c:c + 1]

        def w_qkv(l, kt, c0, c1):
            return w_sb[l % 2][:, O_QKV + kt * 3 * D + c0:O_QKV + kt * 3 * D + c1]

        def w_o(l, kt):
            return w_sb[l % 2][:, O_O + kt * D:O_O + (kt + 1) * D]

        def w_1(l, kt, j):
            return w_sb[l % 2][:, O_1 + kt * FF + j * P:O_1 + kt * FF + (j + 1) * P]

        def w_2(l, j):
            return w_sb[l % 2][:, O_2 + j * D:O_2 + (j + 1) * D]

        def wait(eng, s, value):
            if not isinstance(value, int) or value > 0:
                eng.wait_ge(s, value)

        def run_steps(eng, step, boundary):
            for l in range(LAYERS):
                step(Step(l * B))
                boundary(l)
                first = 1 if 0 < l < LAYERS - 1 else 3
                for b in range(1, first):
                    step(Step(l * B + b))
                with eng.Fori(0, B - 1 - first, 2) as r:
                    r = nc.s_assert_within(r, 0, B - 3 - first, skip_runtime_bounds_check_because="the loop's last value")
                    step(Step(l * B + first, r))
                    step(Step(l * B + first + 1, r))
                step(Step(l * B + B - 1))

        def split3(ap):
            return ap.rearrange("p (a n) -> p a n", a=2)

        block = ctx.enter_context(nc.Block())

        @block.sync
        def _(sp):
            sp.dma_start(cond_sb[:], cond_t).then_inc(cond_ld, 16)
            sp.dma_start(x_sb[:, 0], x[0].rearrange("(t p) d -> p t d", p=P)).then_inc(x_ld[0], 16)
            sp.dma_start(ada_sb[:], ada[0]).then_inc(ada_ld, 16)
            sp.dma_start(vec[:], vecs).then_inc(vec_ld, 16)
            sp.dma_start(x_sb[:, 1], x[1].rearrange("(t p) d -> p t d", p=P)).then_inc(x_ld[1], 16)
            sp.dma_start(w_sb[0][:, 0:O_O], weights[0][:, 0:O_O]).then_inc(wqkv_ld[0], 16)
            sp.dma_start(row_in[:], rows[0].partition_broadcast(B)).then_inc(row_ld, 16)
            sp.dma_start(w_sb[0][:, O_O:], weights[0][:, O_O:]).then_inc(w_ld[0], 16)
            for t in range(T):
                sp.dma_start(x_sb[:, 2:B, t], x[2:B].rearrange("b (t p) d -> t p b d", p=P)[t]).then_inc(x_ld[2], 16)

            def store_rows(l):
                sp.wait_ge(mod_done, l + 1)
                sp.dma_start(par_dram[l], row_out[:]).then_inc(par_st, 16)

            def next_modulation(l):
                if l < LAYERS:
                    sp.wait_ge(mod_done, l)
                    n = 1 if l == 2 else 3
                    sp.dma_start(ada_sb[:, :, 0:n * 2 * D], ada[l]).then_inc(ada_ld, 16)
                    sp.dma_start(row_in[:], rows[l].partition_broadcast(B)).then_inc(row_ld, 16)

            def spill(a):
                for part, tile, ready in ((0, q_hi, q_hi_sb), (1, q_lo, q_lo_sb), (2, k_hi, k_hi_sb), (3, k_lo, k_lo_sb)):
                    wait(sp, ready, a.count(1, 1))
                    dst = qk_dram[a.par, part].rearrange("r (t j) n -> j r t n", j=4)
                    sp.dma_start(dst, tile[:]).then_inc(qk_spill, 16)

            def stack_q(a):
                wait(sp, qk_spill, a.count(64, 64))
                for quad, part in enumerate((0, 0, 1)):
                    for e in range(2):
                        r0 = quad * 2 * HD + e * HD
                        src = qk_dram[a.par, part, e * HD:(e + 1) * HD]
                        dst = q_stack[a.par][r0:r0 + HD].rearrange("r (p e) n -> r p e n", e=2)[:, :, e, :]
                        sp.dma_start(dst, src).then_inc(stack_ld, 16)

            def stack_k(a):
                for quad, part in enumerate((2, 3, 2)):
                    r0 = quad * 2 * HD
                    sp.dma_start(k_stack[a.par][r0:r0 + 2 * HD], qk_dram[a.par, part]).then_inc(stack_ld, 16)

            stack = (stack_q, stack_k)

            def max_rows(g, half):
                wait(sp, max_sb, g.count(2, half + 1))
                h0 = half * H // 2
                for part in range(2):
                    dst = q_stack[g.par][KB + part:KB + part + 1, h0:h0 + H // 2, :]
                    src = max_t[half][part * H // 2:(part + 1) * H // 2, :]
                    sp.dma_start(dst, src).then_inc(max_ld, 16)

            def step(g):
                a, done = g.ahead(1), g.back(2)
                if a.exists:
                    spill(a)
                max_rows(g, 0)
                sp.wait_ge(par_st, 16 * (g.layer + 1))
                src = par_dram[g.layer].rearrange("b r d -> b (r d)")[bass.ds(g.seq, 1) if g.reg is not None else slice(g.seq, g.seq + 1)]
                sp.dma_start(par_sb[g.par][:].rearrange("p r d -> p (r d)"),
                             src.rearrange("b n -> (b n)").partition_broadcast(P)).then_inc(par_ld, 16)
                if done.exists and done.layer == LAYERS - 1:
                    store(done)
                ahead = a.exists and not (g.off > 0 and HAS_MLP[g.back(1).layer])
                if ahead:
                    stack_q(a)
                max_rows(g, 1)
                if a.exists:
                    for part in stack[ahead:]:
                        part(a)

            def store(c):
                b = c.seq
                if c.reg is None:
                    sp.dma_start(out[b].rearrange("(t p) d -> p t d", p=P), x_sb[:, b]).then_inc(out_st, 16)
                else:
                    dst = out[bass.ds(b, 1)].rearrange("b (t p) d -> p (b t) d", p=P)
                    sp.dma_start(dst, x_sb[:, bass.ds(b, 1)].rearrange("p b t d -> p (b t) d")).then_inc(out_st, 16)

            def boundary(l):
                if l + 1 < LAYERS:
                    wait(sp, x2_done, Step(l * B - 1).count(1, 1))
                    wait(sp, proj_ps, Step(l * B - 1).count(1, 1))
                    sp.wait_ge(mod_done, l + 1)
                    n = O_1 if l + 1 == 2 else WCOLS
                    w = w_sb[(l + 1) % 2]
                    sp.dma_start(w[:, 0:O_O], weights[l + 1][:, 0:O_O]).then_inc(wqkv_ld[l + 1], 16)
                    sp.dma_start(w[:, O_O:n], weights[l + 1][:, O_O:n]).then_inc(w_ld[l + 1], 16)
                    store_rows(l + 1)
                    next_modulation(l + 2)

            spill(Step(0))
            sp.wait_ge(q_filled, 2)
            sp.wait_ge(kv_filled, 4)
            for part in stack:
                part(Step(0))
            store_rows(0)
            next_modulation(1)
            run_steps(sp, step, boundary)
            for i in (Step(STEPS - 2), Step(STEPS - 1)):
                sp.wait_ge(x2_done, i.count(1, 1))
                store(i)
            sp.wait_ge(out_st, 16 * B)

        @block.gpsimd
        def _(pool):
            nc.gpsimd.memset(ident[:], 0.0).then_inc(cleared, 1)
            nc.gpsimd.memset(ident_b[:], 0.0).then_inc(cleared, 1)
            nc.gpsimd.memset(mask_q[:], 0.0).then_inc(cleared, 1)
            nc.gpsimd.memset(mask_k[:], 0.0).then_inc(cleared, 1)
            nc.gpsimd.memset(eps_c[:], EPS).then_inc(consts, 1)
            nc.gpsimd.memset(half_c[:], -0.5).then_inc(consts, 1)
            pool.wait_ge(cleared, 4)
            for m in (ident, ident_b):
                nc.gpsimd.affine_select(out=m[:], in_=m[:], compare_op=ALU.not_equal, fill=1.0, base=0,
                                        pattern=[[-1, P]], channel_multiplier=1).then_inc(consts, 1)
            nc.gpsimd.affine_select(out=mask_q[:], in_=mask_q[:], compare_op=ALU.is_ge, fill=MASKED, base=0,
                                    pattern=[[0, 2], [-1, P]], channel_multiplier=1).then_inc(consts, 1)
            nc.gpsimd.affine_select(out=mask_k[:], in_=mask_k[:], compare_op=ALU.is_ge, fill=MASKED, base=0,
                                    pattern=[[0, 2], [1, P]], channel_multiplier=-1).then_inc(consts, 1)
            pool.wait_ge(consts, 2)

            def fill_stack(i):
                nc.gpsimd.memset(q_stack[i][:], 0.0).then_inc(q_filled, 1)

            def power(i, which, mv_s, veps_s, rstd_s):
                wait(pool, mv_s, i.count(1, 1))
                nc.gpsimd.tensor_tensor(veps[:, which, :], mv[:, which, :, 1], eps_c[:], ALU.add).then_inc(veps_s, 1)
                wait(pool, veps_s, i.count(1, 1))
                nc.gpsimd.tensor_tensor(rstd[:, which, :], veps[:, which, :], half_c[:], ALU.pow).then_inc(rstd_s, 1)

            def addend(c, which, s):
                if which:
                    src = x1[:]
                else:
                    src = (x_sb[:, bass.ds(c.seq, 1)] if c.reg is not None else x_sb[:, c.seq:c.seq + 1])[:, 0]
                row = 2 * which + 1
                nc.gpsimd.tensor_tensor(xg[which][:], src, par_sb[c.par][:, row:row + 1, :].to_broadcast([P, T, D]),
                                        ALU.add).then_inc(s, 1)

            def pick(i, norm, s):
                m = mod[:, i.layer, norm]
                src = m[:, :, :, bass.ds(i.seq, 1)] if i.reg is not None else m[:, :, :, i.seq:i.seq + 1]
                nc.gpsimd.tensor_copy(mod_now[:, norm], src).then_inc(s, 1)

            def step(g):
                c, a, n = g.back(1), g.ahead(1), g.ahead(2)
                if a.exists:
                    if g.off == 0:
                        pool.wait_ge(ht1_sb, 1)
                    pool.wait_ge(mod_cols, a.layer + 1)
                    pick(a, 0, mod1_now)
                if c.exists:
                    power(c, 1, ln2_mv, ln2_veps, ln2_rstd)
                    if c.layer != 2:
                        pick(c, 1, mod2_now)
                    addend(c, 1, xg2)
                wait(pool, par_ld, g.count(16, 16))
                if n.exists:
                    power(n, 0, ln1_mv, ln1_veps, ln1_rstd)
                else:
                    wait(pool, xg2, c.count(1, 1))
                addend(g, 0, xg1)

            power(Step(0), 0, ln1_mv, ln1_veps, ln1_rstd)
            pool.wait_ge(mod_cols, 1)
            pick(Step(0), 0, mod1_now)
            power(Step(1), 0, ln1_mv, ln1_veps, ln1_rstd)
            fill_stack(0)
            fill_stack(1)
            run_steps(pool, step, lambda l: None)
            last = Step(STEPS - 1)
            power(last, 1, ln2_mv, ln2_veps, ln2_rstd)
            pick(last, 1, mod2_now)
            addend(last, 1, xg2)

        @block.scalar
        def _(act):
            act.wait_ge(cond_ld, 16)
            nc.scalar.activation(silu_t[:], cond_sb[:], ACT.Exp, scale=-1.0).then_inc(silu_exp, 1)

            def hi_parts(a):
                l = a.layer
                for which, ps, bank, dst, done in (("bq", q_ps, 0, q_hi, q_hi_sb), ("bk", k_ps, 1, k_hi, k_hi_sb)):
                    wait(act, qk_spill, a.count(64, 0))
                    wait(act, ps, a.count(1, 1))
                    src = split3(dense[bank][:])
                    if QKV_BIAS[l]:
                        for t in range(KT):
                            ins = nc.scalar.activation(dst[:, t].bitcast(F32R), src[:, t], ACT.Identity,
                                                       bias=col(l, which, t))
                    else:
                        ins = nc.scalar.activation(dst[:].bitcast(F32R), src, ACT.Identity)
                    ins.then_inc(done, 1)

            def value_copy(a):
                wait(act, v_ps, a.count(1, 1))
                wait(act, o_ps, a.count(4, 4 - 2 * 4))
                if a.off < 2:
                    act.wait_ge(kv_filled, 4)
                src = o_bank[1][:].rearrange("p (t h d) -> p t h d", t=T, h=H)
                nc.scalar.activation(v_aug[a.par][:, :, :, 0:HD], src, ACT.Copy).then_inc(v_sb, 1)

            def modulate(i, norm, bank, ready, v, dst, done):
                wait(act, ready, v)
                src = split3(bank[:])
                m = mod_now[:, norm]
                for t in range(KT):
                    ins = nc.scalar.activation(dst[:, t], src[:, t], ACT.Identity, scale=m[:, 0, t], bias=m[:, 1, t])
                ins.then_inc(done, 1)

            def modulate1(a):
                wait(act, v_ps, a.count(1, 0))
                wait(act, mod1_now, a.count(1, 1))
                modulate(a, 0, o_bank[1], ht1_ps, a.count(1, 1), ht1, ht1_sb)

            def modulate2(c):
                wait(act, w1_ps, c.mlp(4, 0))
                wait(act, mod2_now, c.mlp(1, 1))
                modulate(c, 1, o_bank[0], ht2_ps, c.mlp(1, 1), ht2, ht2_sb)

            def ao_transposed(c):
                l = c.layer
                wait(act, aot_ps, c.count(1, 1))
                wait(act, proj_ps, c.count(1, 0))
                src = split3(o_bank[0][:])
                for t in range(KT):
                    dst = ao_t[:, t]
                    if l == 1:
                        ins = nc.scalar.activation(dst, src[:, t], ACT.Identity)
                    elif l == 2:
                        ins = nc.scalar.activation(dst, src[:, t], ACT.Identity, scale=D ** -0.5, bias=bv_scaled[:, t:t + 1])
                    else:
                        ins = nc.scalar.activation(dst, src[:, t], ACT.Identity, bias=col(l, "bv", t))
                ins.then_inc(aot_sb, 1)

            def gelus(c):
                l = c.layer
                wait(act, w2_ps, c.mlp(1, 0))
                for i in range(FT // 2):
                    wait(act, w1_ps, c.mlp(4, i + 1))
                    src = split3(dense[i % 2][:])
                    for k in range(2):
                        ins = nc.scalar.activation(hid[:, 2 * i + k], src[:, k], ACT.Gelu, bias=col(l, "b1", 2 * i + k))
                    ins.then_inc(gelu_sb, 1)

            def exps(g):
                l = g.layer
                for p in range(PAIRS):
                    if p % 2 == 0:
                        wait(act, o_ps, g.count(4, p // 2 - 1) if p >= 4 else g.count(4, p // 2 + 3 - 4))
                    for kt in range(T):
                        wait(act, st_ps, g.count(16, 2 * p + kt + 1))
                        q0 = P if CAUSAL[l] and kt else 0
                        src = split3(st_bank[kt][:])[:, :, q0:N]
                        nc.scalar.activation(probs[p % 4][:, kt, :, q0:N], src, ACT.Exp,
                                             scale=SCORE_SCALE[l]).then_inc(p_sb, 1)

            def step(g):
                c, a = g.back(1), g.ahead(1)
                mlp = c.exists and HAS_MLP[c.layer]
                if a.exists:
                    modulate1(a)
                    hi_parts(a)
                if mlp:
                    modulate2(c)
                if a.exists:
                    value_copy(a)
                if mlp:
                    gelus(c)
                exps(g)
                ao_transposed(g)

            act.wait_ge(vec_ld, 16)
            nc.scalar.activation(bv_scaled[:], vec[:, VECS[2, "bv"][0]:VECS[2, "bv"][0] + KT], ACT.Copy,
                                 scale=D ** -0.5).then_inc(silu_exp, 1)
            act.wait_ge(silu_exp, 2)
            first = Step(0)
            modulate1(first)
            hi_parts(first)
            value_copy(first)
            run_steps(act, step, lambda l: None)
            modulate2(Step(STEPS - 1))
            gelus(Step(STEPS - 1))

        @block.vector
        def _(dve):
            def fill_stack(i):
                nc.vector.memset(k_stack[i][:], 1.0).then_inc(kv_filled, 1)
                nc.vector.memset(v_aug[i][:], 1.0).then_inc(kv_filled, 1)

            fill_stack(0)

            dve.wait_ge(silu_exp, 1)
            nc.vector.tensor_scalar(silu_t[:], silu_t[:], 1.0, None, ALU.add).then_inc(silu_chain, 1)
            dve.wait_ge(silu_chain, 1)
            nc.vector.reciprocal(silu_t[:], silu_t[:]).then_inc(silu_chain, 1)
            dve.wait_ge(silu_chain, 2)
            nc.vector.tensor_tensor(silu_sb[:], cond_sb[:], silu_t[:], ALU.mult).then_inc(silu_done, 1)

            chained = [0]

            def link(ins):
                chained[0] += 1
                ins.then_inc(mod_chain, 1)
                dve.wait_ge(mod_chain, chained[0])

            def modulation_cols(l):
                dve.wait_ge(vec_ld, 16)
                dve.wait_ge(mod_ps, 2 * l + 1)
                cols = dense[1][:, 0:64].rearrange("p (c b) -> p c b", b=B)
                if l == 2:
                    for t in range(KT):
                        gam, bet = cols[:, t], cols[:, KT + t]
                        link(nc.vector.tensor_scalar(mod_t[:, t], gam, col(l, "bg", t), None, ALU.add))
                        nc.vector.tensor_scalar(mod[:, l, 0, 0, t], mod_t[:, t], col(l, "lg", t), None, ALU.mult)
                        link(nc.vector.tensor_scalar(mod_t[:, t], mod_t[:, t], col(l, "lb", t), None, ALU.mult))
                        ins = nc.vector.scalar_tensor_tensor(mod[:, l, 0, 1, t], bet, col(l, "bb", t), mod_t[:, t],
                                                             ALU.add, ALU.add)
                        if t < KT - 1:
                            link(ins)
                else:
                    for ln in range(2):
                        for t in range(KT):
                            i = 4 * ln + t
                            v0 = 6 * ln + t
                            shift, scale = cols[:, i], cols[:, i + KT]
                            fac, add = mod[:, l, ln, 0, t], mod[:, l, ln, 1, t]
                            link(nc.vector.tensor_scalar(fac, scale, col(l, "ada", v0 + KT), 1.0, ALU.add, ALU.add))
                            if l == 0:
                                ins = nc.vector.tensor_scalar(add, shift, col(l, "ada", v0), None, ALU.add)
                            else:
                                g_, be_ = col(l, f"g{ln + 1}", t), col(l, f"be{ln + 1}", t)
                                link(nc.vector.tensor_scalar(mod_t[:, t], fac, be_, col(l, "ada", v0), ALU.mult, ALU.add))
                                link(nc.vector.tensor_tensor(add, shift, mod_t[:, t], ALU.add))
                                ins = nc.vector.tensor_scalar(fac, fac, g_, None, ALU.mult)
                            if (ln, t) != (1, KT - 1):
                                link(ins)
                ins.then_inc(mod_cols, 1)
                dve.wait_ge(mod_cols, l + 1)

            def modulation_rows(l):
                dve.wait_ge(row_ld, 16 * (l + 1))
                if l > 0:
                    dve.wait_ge(par_st, 16 * l)
                dve.wait_ge(mod_ps, 2 * l + 2)
                r = dense[1][0:B, :].rearrange("p (a d) -> p a d", a=2)
                if l == 2:
                    link(nc.vector.tensor_tensor(row_t[:, 0], r[:, 0], row_in[:, 0], ALU.add))
                    nc.vector.tensor_tensor(row_out[:, 2], row_t[:, 0], row_in[:, 1], ALU.mult)
                    nc.vector.tensor_copy(row_out[:, 0], row_in[:, 4])
                    nc.vector.tensor_copy(row_out[:, 1], row_in[:, 4])
                    link(nc.vector.tensor_tensor(row_t[:, 1], r[:, 1], row_in[:, 2], ALU.add))
                    link(nc.vector.tensor_tensor(row_t[:, 0], row_t[:, 0], row_in[:, 3], ALU.mult))
                    nc.vector.tensor_tensor(row_out[:, 3], row_t[:, 0], row_t[:, 1], ALU.add).then_inc(mod_done, 1)
                else:
                    link(nc.vector.tensor_tensor(row_out[:, 0], r[:, 0], row_in[:, 0], ALU.add))
                    link(nc.vector.tensor_tensor(row_out[:, 2], r[:, 1], row_in[:, 2], ALU.add))
                    nc.vector.tensor_tensor(row_out[:, 1], row_out[:, 0], row_in[:, 1], ALU.mult)
                    nc.vector.tensor_tensor(row_out[:, 3], row_out[:, 2], row_in[:, 3], ALU.mult).then_inc(mod_done, 1)
                dve.wait_ge(mod_done, l + 1)

            def x_of(i):
                return x_sb[:, bass.ds(i.wrapped_seq, 1)][:, 0] if i.reg is not None else x_sb[:, i.seq]

            def norm_stats(src, which, s):
                for t in range(T):
                    ins = nc.vector.bn_stats(stats[:, which, t], src[:, t])
                ins.then_inc(s, 1)

            def norm_mv(which, s):
                for t in range(T):
                    ins = nc.vector.bn_aggr(mv[:, which, t], stats[:, which, t])
                ins.then_inc(s, 1)

            def normalize(i, src, which, rstd_s, dst, s):
                wait(dve, rstd_s, i.count(1, 1))
                for t in range(T):
                    ins = nc.vector.tensor_scalar(dst[:, t], src[:, t], mv[:, which, t, 0:1], rstd[:, which, t:t + 1],
                                                  ALU.subtract, ALU.mult)
                ins.then_inc(s, 1)

            def ln1_a(i):
                if i.layer == 0:
                    for q in range(3):
                        if q <= min(i.off, 2):
                            dve.wait_ge(x_ld[q], 32 if q == 2 else 16)
                norm_stats(x_of(i), 0, ln1_stats)

            def ln1_c(i):
                wait(dve, ht1_ps, i.count(1, 0))
                normalize(i, x_of(i), 0, ln1_rstd, xn1, xn1_done)

            def score_max(g, j):
                p, qt = j // 2, j % 2
                wait(dve, s_ps, g.count(16, j + 1))
                bank = s_bank[(j + (j >= 8)) % 2]
                k1 = P if CAUSAL[g.layer] and qt == 0 else N
                nc.vector.tensor_reduce(neg_max[:, qt, 2 * p:2 * p + 2], split3(bank[:])[:, :, 0:k1], AX.X, ALU.max,
                                        negate=True).then_inc(s_max, 1)

            def max_split(g, half):
                h0 = half * H // 2
                hi = max_parts[:, half, :, 0]
                lo = max_parts[:, half, :, 1]
                src = neg_max[:, :, h0:h0 + H // 2]
                wait(dve, max_ps, g.count(2, half + 1 - 2))
                wait(dve, s_max, g.count(16, 8 * half + 8))
                nc.vector.tensor_copy(hi.bitcast(F32R), src).then_inc(max_hi, 1)
                wait(dve, max_hi, g.count(2, half + 1))
                nc.vector.tensor_tensor(lo.bitcast(F32R), src, hi, ALU.subtract).then_inc(max_lo, 1)

            def max_copy(g, half):
                wait(dve, max_ps, g.count(2, half + 1))
                wait(dve, max_ld, g.count(64, 32 * half + 32 - 64))
                nc.vector.tensor_copy(max_t[half][:], s_bank[half % 2][0:H, 0:N]).then_inc(max_sb, 1)

            def lo_part(a, which, bank, ready, hi, dst, s):
                l = a.layer
                wait(dve, qk_spill, a.count(64, 0))
                wait(dve, ready, a.count(1, 1))
                src = split3(dense[bank][:])
                if QKV_BIAS[l]:
                    for t in range(KT):
                        ins = nc.vector.scalar_tensor_tensor(dst[:, t].bitcast(F32R), src[:, t], col(l, which, t), hi[:, t],
                                                             ALU.add, ALU.subtract)
                else:
                    ins = nc.vector.tensor_tensor(dst[:].bitcast(F32R), src, hi[:], ALU.subtract)
                ins.then_inc(s, 1)

            def times_gate(c, src, row, s):
                for t in range(T):
                    ins = nc.vector.tensor_tensor(prod[:, t], src[:, t], par_sb[c.par][:, row], ALU.mult)
                ins.then_inc(s, 1)

            def residual(c, dst, src, which, ready, s):
                wait(dve, ready, c.count(1, 1))
                nc.vector.tensor_tensor(dst, src, xg[which][:], ALU.add).then_inc(s, 1)

            def first_residual(c):
                wait(dve, proj_ps, c.count(1, 1))
                wait(dve, par_ld, c.count(16, 16))
                if c.layer == 2:
                    residual(c, x1[:], split3(o_bank[0][:]), 0, xg1, x1_done)
                else:
                    times_gate(c, split3(o_bank[0][:]), 0, prod1)
                    wait(dve, prod1, c.mlp(1, 1))
                    residual(c, x1[:], prod[:], 0, xg1, x1_done)

            def second_residual(c):
                if c.layer == 2:
                    wait(dve, xn2_done, c.count(1, 1))
                    times_gate(c, xn2, 2, prod2)
                else:
                    wait(dve, w2_ps, c.mlp(1, 1))
                    times_gate(c, split3(dense[0][:]), 2, prod2)
                wait(dve, prod2, c.count(1, 1))
                residual(c, x_of(c), prod[:], 1, xg2, x2_done)

            def out_copy(g, q):
                wait(dve, o_ps, g.count(4, q + 1))
                wait(dve, ot_ps, g.count(4, q + 1 - 2))
                nc.vector.tensor_copy(o_sb[q % 2][:], o_bank[q % 2][:, 0:N]).then_inc(o_copy, 1)

            def out_norm(g, q):
                wait(dve, ot_ps, g.count(4, q + 1))
                o4 = o_bank[q % 2][:, N:2 * N].rearrange("p (t h d) -> p t h d", t=T, h=4)
                wait(dve, ao_sb, g.count(4, q))
                nc.vector.reciprocal(rec[:], o4[:, :, :, HD]).then_inc(rec_sb, 1)
                wait(dve, rec_sb, g.count(4, q + 1))
                if q == 0:
                    wait(dve, aot_ps, g.count(1, 0))
                dst = ao[:, :, 4 * HD * q:4 * HD * (q + 1)].rearrange("p t (h d) -> p t h d", h=4)
                nc.vector.tensor_tensor(dst, o4[:, :, :, 0:HD],
                                        rec[:].unsqueeze(3).to_broadcast([P, T, 4, HD]), ALU.mult).then_inc(ao_sb, 1)

            def step(g):
                c, a, n = g.back(1), g.ahead(1), g.ahead(2)
                mlp = c.exists and HAS_MLP[c.layer]
                next_modulation = g.off % B == 0 and g.layer < LAYERS - 1
                if g.off == 0:
                    lo_parts(a)
                score_max(g, 0)
                score_max(g, 1)
                score_max(g, 2)
                if c.exists:
                    first_residual(c)
                    wait(dve, x1_done, c.count(1, 1))
                    norm_stats(x1, 1, ln2_stats)
                    wait(dve, ln2_stats, c.count(1, 1))
                score_max(g, 3)
                if c.exists:
                    norm_mv(1, ln2_mv)
                score_max(g, 4)
                if a.exists and g.off > 0:
                    lo_part(a, "bq", 0, q_hi_sb, q_hi, q_lo, q_lo_sb)
                if c.exists:
                    if mlp:
                        wait(dve, ht2_ps, c.mlp(1, 0))
                    normalize(c, x1, 1, ln2_rstd, xn2, xn2_done)
                score_max(g, 5)
                if a.exists and g.off > 0:
                    lo_part(a, "bk", 1, k_hi_sb, k_hi, k_lo, k_lo_sb)
                score_max(g, 6)
                score_max(g, 7)
                max_split(g, 0)
                max_copy(g, 0)
                for j in range(8, 16):
                    score_max(g, j)
                max_split(g, 1)
                max_copy(g, 1)
                out_copy(g, 0)
                if n.exists:
                    ln1_a(n)
                    wait(dve, ln1_stats, n.count(1, 1))
                out_copy(g, 1)
                if n.exists:
                    norm_mv(0, ln1_mv)
                out_norm(g, 0)
                if n.exists:
                    ln1_c(n)
                out_norm(g, 1)
                out_copy(g, 2)
                out_norm(g, 2)
                if next_modulation:
                    modulation_cols(g.layer + 1)
                out_copy(g, 3)
                out_norm(g, 3)
                if next_modulation:
                    modulation_rows(g.layer + 1)
                if c.exists:
                    second_residual(c)

            def lo_parts(a):
                lo_part(a, "bq", 0, q_hi_sb, q_hi, q_lo, q_lo_sb)
                lo_part(a, "bk", 1, k_hi_sb, k_hi, k_lo, k_lo_sb)

            def first_norm(i):
                ln1_a(i)
                dve.wait_ge(ln1_stats, i.off + 1)
                norm_mv(0, ln1_mv)
                ln1_c(i)

            first_norm(Step(0))
            fill_stack(1)
            modulation_cols(0)
            first_norm(Step(1))
            lo_parts(Step(0))
            modulation_rows(0)
            run_steps(dve, step, lambda l: None)
            last = Step(STEPS - 1)
            dve.wait_ge(x2_done, last.count(1, 0))
            first_residual(last)
            wait(dve, x1_done, last.count(1, 1))
            norm_stats(x1, 1, ln2_stats)
            dve.wait_ge(ln2_stats, last.count(1, 1))
            norm_mv(1, ln2_mv)
            normalize(last, x1, 1, ln2_rstd, xn2, xn2_done)
            second_residual(last)

        @block.tensor
        def _(pe):
            mm, tr = nc.tensor.matmul, nc.tensor.transpose

            def modulation_cols(l):
                pe.wait_ge(ada_ld, 16 * (l + 1))
                pe.wait_ge(cond_ld, 16)
                if l in (1, 3):
                    pe.wait_ge(silu_done, 1)
                cs = silu_sb if l in (1, 3) else cond_sb
                chunks = [k * 2 + t for k in ((0, 1) if l == 2 else (0, 1, 3, 4)) for t in range(KT)]
                for i, ch in enumerate(chunks):
                    for kt in range(KT):
                        ins = mm(dense[1][:, i * B:(i + 1) * B], ada_cols(l, kt, ch * P, (ch + 1) * P), cs[:, kt],
                                 start=kt == 0, stop=kt == KT - 1)
                ins.then_inc(mod_ps, 1)

            def modulation_rows(l):
                pe.wait_ge(mod_cols, l + 1)
                cs = silu_sb if l in (1, 3) else cond_sb
                for i, ch in enumerate((0, 1) if l == 2 else (2, 5)):
                    for kt in range(KT):
                        ins = mm(dense[1][0:B, i * D:(i + 1) * D], cs[:, kt], ada_cols(l, kt, ch * D, (ch + 1) * D),
                                 start=kt == 0, stop=kt == KT - 1)
                ins.then_inc(mod_ps, 1)

            def ada_cols(l, kt, c0, c1):
                return ada_sb[:, kt, c0:c1]

            def transposed(bank, src, ready):
                for t in range(T):
                    for kt in range(KT):
                        ins = tr(bank[:, kt * N + t * P:kt * N + (t + 1) * P], src[:, t, kt * P:(kt + 1) * P], ident[:])
                ins.then_inc(ready, 1)

            def ht1_t(a):
                wait(pe, xn1_done, a.count(1, 1))
                wait(pe, v_sb, a.count(1, 0))
                wait(pe, ao_sb, a.count(4, 4 - 2 * 4))
                transposed(o_bank[1], xn1, ht1_ps)

            def q_product(a):
                pe.wait_ge(wqkv_ld[a.layer], 16)
                wait(pe, ht1_sb, a.count(1, 1))
                wait(pe, q_lo_sb, a.count(1, 0))
                c = a.back(2)
                if c.off > 0 or c.reg is not None:
                    wait(pe, prod2, c.count(1, 0))
                qk_product(a, 0, 0, q_ps)

            def qk_product(a, which, bank, ready):
                for t in range(KT):
                    for kt in range(KT):
                        c0 = which * D + t * P
                        ins = mm(dense[bank][:, t * N:(t + 1) * N], w_qkv(a.layer, kt, c0, c0 + P), ht1[:, kt],
                                 start=kt == 0, stop=kt == KT - 1)
                ins.then_inc(ready, 1)

            def k_product(a):
                wait(pe, k_lo_sb, a.count(1, 0))
                qk_product(a, 1, 1, k_ps)

            def v_product(a, t):
                for kt in range(KT):
                    ins = mm(o_bank[1][:, t * D:(t + 1) * D], ht1[:, kt, t * P:(t + 1) * P],
                             w_qkv(a.layer, kt, 2 * D, 3 * D), start=kt == 0, stop=kt == KT - 1)
                if t == T - 1:
                    ins.then_inc(v_ps, 1)

            def ao_turn(g):
                wait(pe, ao_sb, g.count(4, 4))
                transposed(o_bank[0], ao, aot_ps)

            def projection(c, t):
                if t == 0:
                    pe.wait_ge(w_ld[c.layer], 16)
                    wait(pe, aot_sb, c.count(1, 1))
                for kt in range(KT):
                    ins = mm(o_bank[0][:, t * D:(t + 1) * D], ao_t[:, kt, t * P:(t + 1) * P], w_o(c.layer, kt),
                             start=kt == 0, stop=kt == KT - 1)
                if t == T - 1:
                    ins.then_inc(proj_ps, 1)

            def ht2_t(c, a):
                wait(pe, xn2_done, c.count(1, 1))
                transposed(o_bank[0], xn2, ht2_ps)

            def mlp_up(c, a, i, k):
                if k == 0:
                    if i == 0:
                        wait(pe, ht2_sb, c.mlp(1, 1))
                        if a is not None and a.exists:
                            wait(pe, q_lo_sb, a.count(1, 1))
                    elif i == 1:
                        if a is not None and a.exists:
                            wait(pe, k_lo_sb, a.count(1, 1))
                    else:
                        wait(pe, gelu_sb, c.mlp(4, i - 1))
                for kt in range(KT):
                    ins = mm(dense[i % 2][:, k * N:(k + 1) * N], w_1(c.layer, kt, 2 * i + k), ht2[:, kt],
                             start=kt == 0, stop=kt == KT - 1)
                if k == 1:
                    ins.then_inc(w1_ps, 1)

            def mlp_down(c, lo, hi):
                for i in range(lo, hi):
                    t, j = i // FT, i % FT
                    if i == 0:
                        wait(pe, gelu_sb, c.mlp(4, 3))
                    if i == 6:
                        wait(pe, gelu_sb, c.mlp(4, 4))
                    ins = mm(dense[0][:, t * D:(t + 1) * D], hid[:, j, t * P:(t + 1) * P], w_2(c.layer, j),
                             start=j == 0, stop=j == FT - 1)
                    if i == T * FT - 1:
                        ins.then_inc(w2_ps, 1)

            def score(g, *tiles):
                for j in tiles:
                    p, qt = j // 2, j % 2
                    pos = j + (j >= 8)
                    if j == 0:
                        wait(pe, stack_ld, g.count(144, 144))
                        wait(pe, s_max, g.count(16, 0))
                    elif j == 1:
                        wait(pe, max_sb, g.count(2, 0))
                    elif j == 9:
                        wait(pe, max_sb, g.count(2, 1))
                    elif j == 8:
                        wait(pe, s_max, g.count(16, 8))
                    else:
                        wait(pe, s_max, g.count(16, j - 1))
                    bank = s_bank[pos % 2]
                    causal = CAUSAL[g.layer]
                    k1 = P if causal and qt == 0 else N
                    for e in range(2):
                        ins = mm(bank[:, e * N:e * N + k1],
                                 q_stack[g.par][0:KB, 2 * p + e, qt * P:(qt + 1) * P].bitcast(F32R),
                                 k_stack[g.par][0:KB, p, 0:k1].bitcast(F32R), start=True, stop=not causal)
                        if causal:
                            ins = mm(bank[:, e * N + k1 - P:e * N + k1], ident_b[:], mask_q[:, 0], start=False, stop=True)
                    ins.then_inc(s_ps, 1)

            def max_turn(g, half):
                wait(pe, max_lo, g.count(2, half + 1))
                wait(pe, s_max, g.count(16, 7 if half == 0 else 16))
                for qt in range(T):
                    ins = tr(s_bank[half % 2][0:H, qt * P:(qt + 1) * P],
                             max_parts[:, half, qt].rearrange("p a h -> p (a h)"), ident[:])
                ins.then_inc(max_ps, 1)

            def score_t(g, *pairs):
                for p in pairs:
                    if p == 0:
                        wait(pe, max_ld, g.count(64, 32))
                    if p == PAIRS // 2:
                        wait(pe, max_ld, g.count(64, 64))
                    for kt in range(T):
                        wait(pe, p_sb, g.count(16, 2 * p + kt - 1))
                        causal = CAUSAL[g.layer]
                        q0 = P if causal and kt else 0
                        bank = split3(st_bank[kt][:])
                        ins = mm(bank[:, :, q0:N], k_stack[g.par][0:KM, p, kt * P:(kt + 1) * P].bitcast(F32R),
                                 q_stack[g.par][0:KM, 2 * p:2 * p + 2, q0:N].bitcast(F32R), start=True, stop=not causal)
                        if causal:
                            ins = mm(bank[:, :, kt * P:(kt + 1) * P], ident_b[:], mask_k[:], start=False, stop=True)
                        ins.then_inc(st_ps, 1)

            def values(g, q):
                if q == 0:
                    wait(pe, v_sb, g.count(1, 1))
                if q == 0 and g.off > 0:
                    wait(pe, x1_done, g.count(1, 0))
                    if HAS_MLP[g.back(1).layer]:
                        wait(pe, ht2_sb, g.back(1).mlp(1, 1))
                elif q == 1:
                    if g.ahead(1).exists:
                        wait(pe, v_sb, g.count(1, 2))
                elif q > 1:
                    wait(pe, ao_sb, g.count(4, q - 1))
                wait(pe, p_sb, g.count(16, 4 * q + 4))
                for kt in range(T):
                    q0 = P if CAUSAL[g.layer] and kt else 0
                    for j in range(4):
                        pr = probs[(2 * q + j // 2) % 4]
                        ins = mm(o_bank[q % 2][32 * j:32 * j + 32, q0:N], v_aug[g.par][:, kt, 4 * q + j, :],
                                 pr[:, kt, j % 2, q0:N], start=kt == 0, stop=kt == T - 1)
                ins.then_inc(o_ps, 1)

            def out_turn(g, q):
                wait(pe, o_copy, g.count(4, q + 1))
                for t in range(T):
                    ins = tr(o_bank[q % 2][:, N + t * P:N + (t + 1) * P], o_sb[q % 2][:, t * P:(t + 1) * P], ident[:])
                ins.then_inc(ot_ps, 1)

            def step(g):
                c, a = g.back(1), g.ahead(1)
                mlp = c.exists and HAS_MLP[c.layer]

                def down(lo, hi):
                    if mlp:
                        mlp_down(c, lo, hi)

                next_modulation = g.off % B == 0 and g.layer < LAYERS - 1
                if a.exists:
                    ht1_t(a)
                if g.off == 0:
                    products(a)
                score(g, 0, 1)
                if c.exists:
                    projection(c, 0)
                score(g, 2)
                if c.exists:
                    projection(c, 1)
                score(g, 3)
                if a.exists and g.off > 0:
                    q_product(a)
                score(g, 4)
                if a.exists and g.off > 0:
                    k_product(a)
                score(g, 5)
                if a.exists and g.off > 0:
                    v_product(a, 0)
                    v_product(a, 1)
                score(g, 6)
                if mlp:
                    ht2_t(c, a)
                    score(g, 7)
                    mlp_up(c, a, 0, 0)
                    score(g, 8)
                    mlp_up(c, a, 0, 1)
                    max_turn(g, 0)
                    score(g, 9)
                    mlp_up(c, a, 1, 0)
                    score(g, 10)
                    mlp_up(c, a, 1, 1)
                    score(g, 11)
                    mlp_up(c, a, 2, 0)
                    score(g, 12)
                    mlp_up(c, a, 2, 1)
                    score(g, 13)
                    mlp_up(c, a, 3, 0)
                    score(g, 14)
                    mlp_up(c, a, 3, 1)
                    score(g, 15)
                    down(0, 1)
                    score_t(g, 0)
                    down(1, 3)
                    max_turn(g, 1)
                    down(3, 5)
                    score_t(g, 1)
                    down(5, 7)
                    score_t(g, 2)
                    values(g, 0)
                    score_t(g, 3)
                else:
                    score(g, 7, 8)
                    max_turn(g, 0)
                    score(g, 9, 10, 11, 12)
                    score_t(g, 0)
                    score(g, 13)
                    score_t(g, 1)
                    score(g, 14, 15)
                    score_t(g, 2)
                    max_turn(g, 1)
                    values(g, 0)
                    score_t(g, 3)
                down(7, 8)
                out_turn(g, 0)
                if not mlp:
                    values(g, 1)
                    out_turn(g, 1)
                score_t(g, 4)
                if mlp:
                    values(g, 1)
                score_t(g, 5)
                down(8, 9)
                if mlp:
                    out_turn(g, 1)
                score_t(g, 6)
                values(g, 2)
                score_t(g, 7)
                down(9, 10)
                out_turn(g, 2)
                if next_modulation:
                    if not mlp:
                        wait(pe, k_lo_sb, a.count(1, 1))
                    modulation_cols(g.layer + 1)
                down(10, 11)
                values(g, 3)
                down(11, 13)
                out_turn(g, 3)
                down(13, 16)
                if next_modulation:
                    modulation_rows(g.layer + 1)
                ao_turn(g)

            def boundary(l):
                if l + 1 < LAYERS:
                    pe.wait_ge(mod_done, l + 2)

            def products(a):
                q_product(a)
                k_product(a)
                for t in range(T):
                    v_product(a, t)

            pe.wait_ge(consts, 6)
            modulation_cols(0)
            first = Step(0)
            ht1_t(first)
            pe.wait_ge(mod_cols, 1)
            products(first)
            pe.wait_ge(k_lo_sb, 1)
            modulation_rows(0)
            pe.wait_ge(mod_done, 1)
            run_steps(pe, step, boundary)
            last = Step(STEPS - 1)
            for t in range(T):
                projection(last, t)
            ht2_t(last, None)
            for i in range(FT // 2):
                for k in range(2):
                    mlp_up(last, None, i, k)
            mlp_down(last, 0, T * FT)


def _pack(inputs):
    g = {k: np.asarray(v) for k, v in inputs.items()}

    def tiles(w):
        return w.reshape(-1, P, w.shape[1]).transpose(1, 0, 2)

    def L(l, name):
        return g[f"L{l}_cond_{name}"]

    qkv2 = L(2, "Wqkv").reshape(D, 3, D).transpose(2, 1, 0).reshape(D, 3 * D)
    bqkv2 = L(2, "bqkv").reshape(D, 3).T
    weights = [
        (np.concatenate([L(0, "Wq"), L(0, "Wk"), L(0, "Wv")], 1), L(0, "Wo"), L(0, "W1"), L(0, "W2")),
        (L(1, "Wqkv"), L(1, "Wproj"), L(1, "W1"), L(1, "W2")),
        (qkv2, L(2, "Wp").T),
        (L(3, "Wqkv"), L(3, "Wproj"), L(3, "W1"), L(3, "W2")),
    ]
    ada = [L(0, "W_ada"), L(1, "Wada"), np.concatenate([L(2, "Wg").T, L(2, "Wb").T], 1), L(3, "Wt")]
    biases = (L(0, "b_ada"), L(1, "bada"), None, L(3, "bt"))
    vec = {
        (0, "ada"): biases[0], (0, "bq"): L(0, "bq"), (0, "bk"): L(0, "bk"), (0, "bv"): L(0, "bv"), (0, "b1"): L(0, "b1"),
        (1, "ada"): biases[1], (1, "b1"): L(1, "b1"),
        (2, "lg"): L(2, "ln_g"), (2, "lb"): L(2, "ln_b"), (2, "bg"): L(2, "bg"), (2, "bb"): L(2, "bb"),
        (2, "bq"): bqkv2[0], (2, "bk"): bqkv2[1], (2, "bv"): bqkv2[2],
        (3, "ada"): biases[3], (3, "bq"): L(3, "bqkv")[0:D], (3, "bk"): L(3, "bqkv")[D:2 * D],
        (3, "bv"): L(3, "bqkv")[2 * D:], (3, "b1"): L(3, "b1"),
    }
    for l in (1, 3):
        for n in ("g1", "be1", "g2", "be2"):
            vec[l, n] = L(l, n)
    vecs = np.concatenate([vec[k].reshape(-1, P) for k in VECS], 0).T
    rows = []
    for l in range(LAYERS):
        if l == 2:
            r = [L(2, "bg"), L(2, "ln_g"), L(2, "bb"), L(2, "ln_b"), L(2, "bp")]
        else:
            bo, b2 = L(l, "bo" if l == 0 else "bproj"), L(l, "b2")
            r = [biases[l][2 * D:3 * D], bo, biases[l][5 * D:], b2, b2]
        rows.append(np.stack(r))
    packed = {"x": g["x"], "cond_t": g["cond_1024"].T.reshape(KT, P, B).transpose(1, 0, 2), "vecs": vecs,
              "rows": np.stack(rows)}
    for l in range(LAYERS):
        packed[f"ada{l}"] = tiles(ada[l])
        packed[f"w{l}"] = np.concatenate([tiles(w).reshape(P, -1) for w in weights[l]], 1)
    return {k: np.ascontiguousarray(v) for k, v in packed.items()}


def kernel(**inputs):
    import concourse.bacc as _bacc
    from concourse.bass_utils import run_bass_kernel_spmd as _run

    nc = _bacc.Bacc("TRN2", target_bir_lowering=False, num_devices=1)
    arrays = _pack(inputs)
    t = {k: nc.dram_tensor(k, a.shape, mybir.dt.from_np(a.dtype), kind="ExternalInput").ap() for k, a in arrays.items()}
    out = nc.dram_tensor("out", (B, N, D), F32, kind="ExternalOutput").ap()
    cond_seq_blocks(nc, t["x"], t["cond_t"], t["vecs"], t["rows"], [t[f"ada{l}"] for l in range(LAYERS)],
                    [t[f"w{l}"] for l in range(LAYERS)], out)
    return _run(nc, [arrays], core_ids=[0]).results[0]["out"]
```

```python
from contextlib import ExitStack

import numpy as np

import concourse.bass as bass
from concourse import mybir

P = 128
B, N, D, H, FF = 8, 256, 256, 16, 1024
HD = D // H
T = N // P
KT = D // P
FT = FF // P
PAIRS = H // 2
LAYERS = 4
STEPS = LAYERS * B
HAS_MLP = (True, True, False, True)
CAUSAL = (False, True, False, False)
QKV_BIAS = (True, False, True, True)
SCORE_SCALE = (HD ** -0.5, HD ** -0.5, 1.0, HD ** -0.5)
MOD_STEP = (0, B, 2 * B + 1)
EPS = 1e-5
MASKED = -1e30
KB = 3 * 2 * HD
KM = KB + 2

F32 = mybir.dt.float32
F32R = mybir.dt.float32r
BF16 = mybir.dt.bfloat16
ALU = mybir.AluOpType
ACT = mybir.ActivationFunctionType
AX = mybir.AxisListType

VECS = {}
for _l, _names in enumerate((
    (("ada", 12), ("bq", 2), ("bk", 2), ("bv", 2), ("b1", 8)),
    (("ada", 12), ("g1", 2), ("be1", 2), ("g2", 2), ("be2", 2), ("b1", 8)),
    (("lg", 2), ("lb", 2), ("bg", 2), ("bb", 2), ("bq", 2), ("bk", 2), ("bv", 2)),
    (("ada", 12), ("g1", 2), ("be1", 2), ("g2", 2), ("be2", 2), ("bq", 2), ("bk", 2), ("bv", 2), ("b1", 8)),
)):
    for _n, _c in _names:
        VECS[_l, _n] = (sum(c for _, c in VECS.values()), _c)
NVEC = sum(c for _, c in VECS.values())

O_QKV, O_O = 0, KT * 3 * D
O_1 = O_O + KT * D
O_2 = O_1 + KT * FF
WCOLS = O_2 + FT * D
ADA = 6 * D
NROW = 5
NPAR = 4


class Step:

    def __init__(self, off, reg=None):
        self.off, self.reg = off, reg
        self.layer, self.par = off // B, off % 2

    def back(self, n):
        return Step(self.off - n, self.reg)

    def ahead(self, n):
        return Step(self.off + n, self.reg)

    @property
    def exists(self):
        return self.reg is not None or 0 <= self.off < STEPS

    @property
    def seq(self):
        b = self.off % B
        return b if self.reg is None else self.reg + b

    @property
    def wrapped_seq(self):
        return self.seq if self.reg is None else (self.reg + self.off % B) % B

    def _value(self, first, per, c):
        value = first * per + c
        if self.reg is None:
            return value
        assert value > 0
        return self.reg * per + value

    def count(self, per, c):
        return self._value(self.off, per, c)

    def mlp(self, per, c):
        return self._value(self.off - (B if self.layer > 2 else 0), per, c)


def cond_seq_blocks(nc, x, cond_t, vecs, rows, ada, weights, out):
    par_dram = nc.dram_tensor("par_dram", (LAYERS, B, NPAR, D), F32).ap()
    qk_dram = nc.dram_tensor("qk_dram", (2, 4, 2 * HD, PAIRS, N), F32).ap()

    with ExitStack() as ctx:
        def sb(name, shape, dt=F32):
            return ctx.enter_context(nc.sbuf_tensor(name, shape, dt))

        def sb_at(name, shape, offset):
            return nc.alloc_sbuf_tensor_at(name, shape, F32, offset=offset)

        def sem(name):
            return ctx.enter_context(nc.semaphore(name))

        first_free = -(-nc.sbuf_base // 32) * 32
        w_at = [first_free + i * WCOLS * 4 for i in range(2)]
        w_sb = [sb(f"w_sb{i}", [P, WCOLS]) for i in range(2)]
        w1_lo = [sb_at(f"w1_lo{i}", [P, KT, FF], w_at[i] + O_1 * 4) for i in range(2)]
        w1_hi = [sb_at(f"w1_hi{i}", [P, KT, FF], w_at[1 - i] + O_2 * 4) for i in range(2)]
        xn2_at = first_free + 2 * WCOLS * 4
        xn2 = sb("xn2", [P, T, D])
        ht2_lo = sb_at("ht2_lo", [P, KT, N], xn2_at)
        x_sb = sb("x_sb", [P, B, T, D])
        ada_sb = sb("ada_sb", [P, KT, ADA])
        vec = sb("vec", [P, NVEC])
        cond_sb = sb("cond_sb", [P, KT, B])
        silu_sb = sb("silu_sb", [P, KT, B])
        silu_t = sb("silu_t", [P, KT, B])
        mod = sb("mod", [P, LAYERS, 2, 2, KT, B])
        mod_now = sb("mod_now", [P, 2, 2, KT, 1])
        mod_t = sb("mod_t", [P, 2, KT, B])
        row_in = sb("row_in", [B, NROW, D])
        row_out = sb("row_out", [B, NPAR, D])
        par_sb = [sb(f"par_sb{i}", [P, NPAR, D]) for i in range(2)]
        q_stack = [sb(f"q_stack{i}", [P, H, N]) for i in range(2)]
        k_stack = [sb(f"k_stack{i}", [P, PAIRS, N]) for i in range(2)]
        v_aug = [sb(f"v_aug{i}", [P, T, H, 2 * HD]) for i in range(2)]
        xn1 = sb("xn1", [P, T, D])
        ht1 = sb("ht1", [P, KT, N])
        ht2 = sb("ht2", [P, KT, N])
        q_hi, q_lo, k_hi, k_lo = (sb(n, [P, KT, N]) for n in ("q_hi", "q_lo", "k_hi", "k_lo"))
        neg_max = sb("neg_max", [P, T, H])
        max_parts = sb("max_parts", [P, 2, T, 2, H // 2])
        max_t = [sb(f"max_t{i}", [H, N]) for i in range(2)]
        probs = [sb(f"probs{i}", [P, T, 2, N]) for i in range(4)]
        o_sb = [sb(f"o_sb{i}", [P, N]) for i in range(2)]
        rec = sb("rec", [P, T, 4])
        bv_scaled = sb("bv_scaled", [P, KT])
        ao = sb("ao", [P, T, D])
        ao_t = sb("ao_t", [P, KT, N])
        hid = sb("hid", [P, FT, N])
        xg = [sb(f"xg{i}", [P, T, D]) for i in range(2)]
        ht2_raw = xn2
        x1 = xg[0]
        prod = sb("prod", [P, T, D])
        row_t = prod[0:B]
        stats = sb("stats", [P, 2, T, 6])
        mv = sb("mv", [P, 2, T, 2])
        veps = sb("veps", [P, 2, T])
        rstd = sb("rstd", [P, 2, T])
        eps_c = sb("eps_c", [P, T])
        half_c = sb("half_c", [P, T])
        table_out = sb("table_out", [P, 1])
        ident = sb("ident", [P, P])
        ident_b = sb("ident_b", [P, P], BF16)
        mask_q = sb("mask_q", [P, 2, P], BF16)
        mask_k = sb("mask_k", [P, 2, P], BF16)

        dense = [ctx.enter_context(nc.psum_tensor(f"dense{i}", [P, 512], F32)) for i in range(2)]
        s_bank = [ctx.enter_context(nc.psum_tensor(f"s_bank{i}", [P, 512], F32)) for i in range(2)]
        st_bank = [ctx.enter_context(nc.psum_tensor(f"st_bank{i}", [P, 512], F32)) for i in range(2)]
        o_bank = [ctx.enter_context(nc.psum_tensor(f"o_bank{i}", [P, 512], F32)) for i in range(2)]

        cond_ld, vec_ld, row_ld, ada_first_ld, ada_ld = (
            sem(n) for n in ("cond_ld", "vec_ld", "row_ld", "ada_first_ld", "ada_ld"))
        wqkv_ld = [sem(f"wqkv_ld{l}") for l in range(LAYERS)]
        w_ld = [sem(f"w_ld{l}") for l in range(LAYERS)]
        w2_ld = [sem(f"w2_ld{l}") for l in range(LAYERS)]
        x_ld = [sem(f"x_ld{i}") for i in range(3)]
        consts, cleared, q_filled, kv_filled = sem("consts"), sem("cleared"), sem("q_filled"), sem("kv_filled")
        mod_cols = sem("mod_cols")
        w1_hi_sb, w1_split = sem("w1_hi_sb"), sem("w1_split")
        silu_exp, silu_chain, silu_done = sem("silu_exp"), sem("silu_chain"), sem("silu_done")
        mod_ps, mod_chain, mod_done, par_st = sem("mod_ps"), sem("mod_chain"), sem("mod_done"), sem("par_st")
        par_ld = sem("par_ld")
        ln1_stats, ln1_mv, ln1_veps, ln1_rstd, xn1_done = (
            sem(n) for n in ("ln1_stats", "ln1_mv", "ln1_veps", "ln1_rstd", "xn1_done"))
        ln2_stats, ln2_mv, ln2_veps, ln2_rstd, xn2_done = (
            sem(n) for n in ("ln2_stats", "ln2_mv", "ln2_veps", "ln2_rstd", "xn2_done"))
        ht1_ps, ht1_sb, q_ps, k_ps, v_ps = (sem(n) for n in ("ht1_ps", "ht1_sb", "q_ps", "k_ps", "v_ps"))
        q_hi_sb, q_lo_sb, k_hi_sb, k_lo_sb, v_sb = (
            sem(n) for n in ("q_hi_sb", "q_lo_sb", "k_hi_sb", "k_lo_sb", "v_sb"))
        q_spill, k_spill, stack_ld = sem("q_spill"), sem("k_spill"), sem("stack_ld")
        s_ps, s_max, max_hi, max_lo, max_ps, max_sb, max_ld = (
            sem(n) for n in ("s_ps", "s_max", "max_hi", "max_lo", "max_ps", "max_sb", "max_ld"))
        st_ps, p_sb, o_ps, o_copy, ot_ps, rec_sb, ao_sb = (
            sem(n) for n in ("st_ps", "p_sb", "o_ps", "o_copy", "ot_ps", "rec_sb", "ao_sb"))
        aot_ps, aot_sb, proj_ps, prod1, xg1, x1_done = (
            sem(n) for n in ("aot_ps", "aot_sb", "proj_ps", "prod1", "xg1", "x1_done"))
        mod1_now, mod2_now = sem("mod1_now"), sem("mod2_now")
        ht2_ps, ht2_raw_sb, ht2_hi_sb, ht2_sb, w1_ps, gelu_sb, w2_ps, prod2, xg2, x2_done = (
            sem(n) for n in ("ht2_ps", "ht2_raw_sb", "ht2_hi_sb", "ht2_sb", "w1_ps", "gelu_sb", "w2_ps", "prod2", "xg2", "x2_done"))
        out_st = sem("out_st")

        def col(l, name, i):
            c = VECS[l, name][0] + i
            return vec[:, c:c + 1]

        def w_qkv(l, kt, c0, c1):
            return w_sb[l % 2][:, O_QKV + kt * 3 * D + c0:O_QKV + kt * 3 * D + c1]

        def w_o(l, kt):
            return w_sb[l % 2][:, O_O + kt * D:O_O + (kt + 1) * D]

        def w_1(l, parts, kt, j):
            return parts[l % 2][:, kt, j * P:(j + 1) * P].bitcast(F32R)

        def w_2(l, j):
            return w_sb[l % 2][:, O_2 + j * D:O_2 + (j + 1) * D]

        def wait(eng, s, value):
            if not isinstance(value, int) or value > 0:
                eng.wait_ge(s, value)

        def inputs_of(a):
            return a.exists and (a.reg is not None or a.off > 1)

        def modulation_of(g):
            return MOD_STEP.index(g.off) + 1 if g.reg is None and g.off in MOD_STEP else None

        def modulations_before(g):
            return 1 + sum(m < g.off for m in MOD_STEP)

        def run_steps(eng, step, after=None):
            def single(g):
                step(g)
                if after:
                    after(g)

            for l in range(LAYERS):
                first = 3
                for b in range(first):
                    single(Step(l * B + b))
                with eng.Fori(0, B - 1 - first, 2) as r:
                    r = nc.s_assert_within(r, 0, B - 3 - first, skip_runtime_bounds_check_because="the loop's last value")
                    step(Step(l * B + first, r))
                    step(Step(l * B + first + 1, r))
                single(Step(l * B + B - 1))

        def max_rows(eng, g, half):
            wait(eng, max_sb, g.count(2, half + 1))
            h0 = half * H // 2
            for part in range(2):
                dst = q_stack[g.par][KB + part:KB + part + 1, h0:h0 + H // 2, :]
                src = max_t[half][part * H // 2:(part + 1) * H // 2, :]
                eng.dma_start(dst, src).then_inc(max_ld, 16)

        def cols_bank(l, norm):
            return s_bank[norm] if l == 0 else dense[0]

        def split3(ap):
            return ap.rearrange("p (a n) -> p a n", a=2)

        block = ctx.enter_context(nc.Block())

        @block.sync
        def _(sp):
            def load_weights(l, c0, c1, loaded):
                sp.dma_start(w_sb[l % 2][:, c0:c1], weights[l][:, c0:c1]).then_inc(loaded[l], 16)

            sp.dma_start(cond_sb[:], cond_t).then_inc(cond_ld, 16)
            sp.dma_start(x_sb[:, 0], x[0].rearrange("(t p) d -> p t d", p=P)).then_inc(x_ld[0], 16)
            sp.dma_start(ada_sb[:, :, 0:2 * D], ada[0][:, :, 0:2 * D]).then_inc(ada_first_ld, 16)
            sp.dma_start(vec[:], vecs).then_inc(vec_ld, 16)
            sp.dma_start(ada_sb[:, :, 2 * D:ADA], ada[0][:, :, 2 * D:ADA]).then_inc(ada_ld, 16)
            sp.dma_start(x_sb[:, 1], x[1].rearrange("(t p) d -> p t d", p=P)).then_inc(x_ld[1], 16)
            load_weights(0, 0, O_O, wqkv_ld)
            sp.dma_start(row_in[:], rows[0].partition_broadcast(B)).then_inc(row_ld, 16)
            load_weights(0, O_O, O_2, w_ld)
            load_weights(0, O_2, WCOLS, w2_ld)
            for t in range(T):
                sp.dma_start(x_sb[:, 2:B, t], x[2:B].rearrange("b (t p) d -> t p b d", p=P)[t]).then_inc(x_ld[2], 16)

            def store_rows(l):
                sp.wait_ge(mod_done, l + 1)
                sp.dma_start(par_dram[l], row_out[:]).then_inc(par_st, 16)

            def next_modulation(l):
                if l < LAYERS:
                    sp.wait_ge(mod_done, l)
                    n = 1 if l == 2 else 3
                    sp.dma_start(ada_sb[:, :, 0:n * 2 * D], ada[l]).then_inc(ada_ld, 16)
                    sp.dma_start(row_in[:], rows[l].partition_broadcast(B)).then_inc(row_ld, 16)

            def spill(a):
                for part, tile, ready in ((0, q_hi, q_hi_sb), (1, q_lo, q_lo_sb), (2, k_hi, k_hi_sb), (3, k_lo, k_lo_sb)):
                    wait(sp, ready, a.count(1, 1))
                    dst = qk_dram[a.par, part].rearrange("r (t j) n -> j r t n", j=4)
                    sp.dma_start(dst, tile[:]).then_inc(q_spill if part < 2 else k_spill, 16)

            def stack(a):
                wait(sp, q_spill, a.count(32, 32))
                for quad, part in enumerate((0, 0, 1)):
                    for e in range(2):
                        r0 = quad * 2 * HD + e * HD
                        src = qk_dram[a.par, part, e * HD:(e + 1) * HD]
                        dst = q_stack[a.par][r0:r0 + HD].rearrange("r (p e) n -> r p e n", e=2)[:, :, e, :]
                        sp.dma_start(dst, src).then_inc(stack_ld, 16)
                wait(sp, k_spill, a.count(32, 32))
                for quad, part in enumerate((2, 3, 2)):
                    r0 = quad * 2 * HD
                    sp.dma_start(k_stack[a.par][r0:r0 + 2 * HD], qk_dram[a.par, part]).then_inc(stack_ld, 16)

            def step(g):
                a, c, done = g.ahead(1), g.back(1), g.back(2)
                mlp = c.exists and HAS_MLP[c.layer]
                if inputs_of(a):
                    spill(a)
                    stack(a)
                if g.reg is None:
                    wait(sp, x2_done, done.count(1, 1))
                sp.wait_ge(par_st, 16 * (g.layer + 1))
                src = par_dram[g.layer].rearrange("b r d -> b (r d)")[bass.ds(g.seq, 1) if g.reg is not None else slice(g.seq, g.seq + 1)]
                sp.dma_start(par_sb[g.par][:].rearrange("p r d -> p (r d)"),
                             src.rearrange("b n -> (b n)").partition_broadcast(P)).then_inc(par_ld, 16)
                if done.exists and done.layer == LAYERS - 1:
                    store(done)
                if mlp:
                    max_rows(sp, g, 1)
                if a.exists and HAS_MLP[g.layer]:
                    max_rows(sp, a, 0)

            def store(c):
                b = c.seq
                if c.reg is None:
                    sp.dma_start(out[b].rearrange("(t p) d -> p t d", p=P), x_sb[:, b]).then_inc(out_st, 16)
                else:
                    dst = out[bass.ds(b, 1)].rearrange("b (t p) d -> p (b t) d", p=P)
                    sp.dma_start(dst, x_sb[:, bass.ds(b, 1)].rearrange("p b t d -> p (b t) d")).then_inc(out_st, 16)

            def after(g):
                l, last_layer = g.layer, g.layer == LAYERS - 1
                if g.off == l * B:
                    wait(sp, x2_done, g.back(1).count(1, 1))
                    if HAS_MLP[l] and l > 0:
                        load_weights(l, O_2, WCOLS, w2_ld)
                    if not last_layer:
                        load_weights(l + 1, 0, O_O, wqkv_ld)
                if modulation_of(g):
                    store_rows(modulation_of(g))
                    next_modulation(modulation_of(g) + 1)
                if g.off == l * B + B - 1 and not last_layer:
                    load_weights(l + 1, O_O, O_2 if HAS_MLP[l + 1] else O_1, w_ld)

            spill(Step(0))
            sp.wait_ge(q_filled, 2)
            sp.wait_ge(kv_filled, 4)
            stack(Step(0))
            store_rows(0)
            spill(Step(1))
            sp.wait_ge(stack_ld, 144)
            stack(Step(1))
            sp.wait_ge(max_ld, 32)
            next_modulation(1)
            run_steps(sp, step, after)
            for i in (Step(STEPS - 2), Step(STEPS - 1)):
                sp.wait_ge(x2_done, i.count(1, 1))
                store(i)
            sp.wait_ge(out_st, 16 * B)

        @block.gpsimd
        def _(pool):
            nc.gpsimd.memset(ident[:], 0.0).then_inc(cleared, 1)
            nc.gpsimd.memset(ident_b[:], 0.0).then_inc(cleared, 1)
            nc.gpsimd.memset(mask_q[:], 0.0).then_inc(cleared, 1)
            nc.gpsimd.memset(mask_k[:], 0.0).then_inc(cleared, 1)
            nc.gpsimd.memset(eps_c[:], EPS).then_inc(consts, 1)
            nc.gpsimd.memset(half_c[:], -0.5).then_inc(consts, 1)
            pool.wait_ge(cleared, 4)
            for m in (ident, ident_b):
                nc.gpsimd.affine_select(out=m[:], in_=m[:], compare_op=ALU.not_equal, fill=1.0, base=0,
                                        pattern=[[-1, P]], channel_multiplier=1).then_inc(consts, 1)
            nc.gpsimd.affine_select(out=mask_q[:], in_=mask_q[:], compare_op=ALU.is_ge, fill=MASKED, base=0,
                                    pattern=[[0, 2], [-1, P]], channel_multiplier=1).then_inc(consts, 1)
            nc.gpsimd.affine_select(out=mask_k[:], in_=mask_k[:], compare_op=ALU.is_ge, fill=MASKED, base=0,
                                    pattern=[[0, 2], [1, P]], channel_multiplier=-1).then_inc(consts, 1)
            pool.wait_ge(consts, 2)

            def fill_stack(i):
                nc.gpsimd.memset(q_stack[i][:], 0.0).then_inc(q_filled, 1)

            def power(i, which, mv_s, veps_s, rstd_s):
                wait(pool, mv_s, i.count(1, 1))
                nc.gpsimd.tensor_tensor(veps[:, which, :], mv[:, which, :, 1], eps_c[:], ALU.add).then_inc(veps_s, 1)
                wait(pool, veps_s, i.count(1, 1))
                nc.gpsimd.tensor_tensor(rstd[:, which, :], veps[:, which, :], half_c[:], ALU.pow).then_inc(rstd_s, 1)

            def addend(c, which, s):
                if which:
                    src = x1[:]
                else:
                    src = (x_sb[:, bass.ds(c.seq, 1)] if c.reg is not None else x_sb[:, c.seq:c.seq + 1])[:, 0]
                row = 2 * which + 1
                nc.gpsimd.tensor_tensor(xg[which][:], src, par_sb[c.par][:, row:row + 1, :].to_broadcast([P, T, D]),
                                        ALU.add).then_inc(s, 1)

            def pick(i, norm, s):
                m = mod[:, i.layer, norm]
                src = m[:, :, :, bass.ds(i.seq, 1)] if i.reg is not None else m[:, :, :, i.seq:i.seq + 1]
                nc.gpsimd.tensor_copy(mod_now[:, norm], src).then_inc(s, 1)

            def split_w1(l):
                before = l - (l > 2)
                pool.wait_ge(w_ld[l], 16)
                if before:
                    pool.wait_ge(w2_ps, before * B)
                for i in range(FT // 2):
                    cols = slice(2 * i * P, 2 * (i + 1) * P)
                    raw = w_sb[l % 2][:, O_1:O_2].rearrange("p (k f) -> p k f", k=KT)[:, :, cols]
                    hi, lo = w1_hi[l % 2][:, :, cols], w1_lo[l % 2][:, :, cols]
                    nc.gpsimd.tensor_copy(hi.bitcast(F32R), raw).then_inc(w1_hi_sb, 1)
                    pool.wait_ge(w1_hi_sb, before * FT // 2 + i + 1)
                    nc.gpsimd.tensor_tensor(lo.bitcast(F32R), raw, hi, ALU.subtract).then_inc(w1_split, 1)

            def step(g):
                c, a, n = g.back(1), g.ahead(1), g.ahead(2)
                if inputs_of(a):
                    pool.wait_ge(mod_cols, 2 * (a.layer + 1))
                    if g.reg is None:
                        wait(pool, ht1_sb, a.count(1, 0))
                    pick(a, 0, mod1_now)
                if c.exists:
                    power(c, 1, ln2_mv, ln2_veps, ln2_rstd)
                    if c.layer != 2:
                        pick(c, 1, mod2_now)
                    addend(c, 1, xg2)
                    if g.reg is None and g.off % B == 1 and g.layer > 0 and HAS_MLP[g.layer]:
                        split_w1(g.layer)
                wait(pool, par_ld, g.count(16, 16))
                if n.exists:
                    power(n, 0, ln1_mv, ln1_veps, ln1_rstd)
                else:
                    wait(pool, xg2, c.count(1, 1))
                    wait(pool, xn2_done, c.count(1, 1))
                addend(g, 0, xg1)

            power(Step(0), 0, ln1_mv, ln1_veps, ln1_rstd)
            pool.wait_ge(mod_cols, 1)
            pick(Step(0), 0, mod1_now)
            power(Step(1), 0, ln1_mv, ln1_veps, ln1_rstd)
            pool.wait_ge(ht1_sb, 1)
            pick(Step(1), 0, mod1_now)
            fill_stack(0)
            fill_stack(1)
            split_w1(0)
            run_steps(pool, step)
            last = Step(STEPS - 1)
            power(last, 1, ln2_mv, ln2_veps, ln2_rstd)
            pick(last, 1, mod2_now)
            addend(last, 1, xg2)

        @block.scalar
        def _(act):
            act.wait_ge(cond_ld, 16)
            nc.scalar.activation(silu_t[:], cond_sb[:], ACT.Exp, scale=-1.0).then_inc(silu_exp, 1)

            def hi_part(a, which, ps, bank, dst, done, spilled):
                wait(act, spilled, a.count(32, 0))
                wait(act, ps, a.count(1, 1))
                src = split3(dense[bank][:])
                if QKV_BIAS[a.layer]:
                    for t in range(KT):
                        ins = nc.scalar.activation(dst[:, t].bitcast(F32R), src[:, t], ACT.Identity,
                                                   bias=col(a.layer, which, t))
                else:
                    ins = nc.scalar.activation(dst[:].bitcast(F32R), src, ACT.Identity)
                ins.then_inc(done, 1)

            def query_hi(a):
                hi_part(a, "bq", q_ps, 0, q_hi, q_hi_sb, q_spill)

            def key_hi(a):
                hi_part(a, "bk", k_ps, 1, k_hi, k_hi_sb, k_spill)

            def value_copy(a):
                wait(act, v_ps, a.count(1, 1))
                wait(act, o_ps, a.count(4, 4 - 2 * 4))
                if a.off < 2:
                    act.wait_ge(kv_filled, 4)
                src = o_bank[1][:].rearrange("p (t h d) -> p t h d", t=T, h=H)
                nc.scalar.activation(v_aug[a.par][:, :, :, 0:HD], src, ACT.Copy).then_inc(v_sb, 1)

            def modulate(i, norm, bank, ready, v, dst, done):
                wait(act, ready, v)
                src = split3(bank[:])
                m = mod_now[:, norm]
                for t in range(KT):
                    ins = nc.scalar.activation(dst[:, t], src[:, t], ACT.Identity, scale=m[:, 0, t], bias=m[:, 1, t])
                ins.then_inc(done, 1)

            def modulate1(a):
                wait(act, v_ps, a.count(1, 0))
                wait(act, mod1_now, a.count(1, 1))
                modulate(a, 0, o_bank[1], ht1_ps, a.count(1, 1), ht1, ht1_sb)

            def modulate2(c):
                wait(act, mod2_now, c.mlp(1, 1))
                modulate(c, 1, dense[0], ht2_ps, c.mlp(1, 1), ht2_raw, ht2_raw_sb)

            def ao_transposed(c):
                l = c.layer
                wait(act, aot_ps, c.count(1, 1))
                wait(act, proj_ps, c.count(1, 0))
                src = split3(o_bank[0][:])
                for t in range(KT):
                    dst = ao_t[:, t]
                    if l == 1:
                        ins = nc.scalar.activation(dst, src[:, t], ACT.Identity)
                    elif l == 2:
                        ins = nc.scalar.activation(dst, src[:, t], ACT.Identity, scale=D ** -0.5, bias=bv_scaled[:, t:t + 1])
                    else:
                        ins = nc.scalar.activation(dst, src[:, t], ACT.Identity, bias=col(l, "bv", t))
                ins.then_inc(aot_sb, 1)

            def bring_table(func):
                nc.scalar.activation(table_out[:], eps_c[:, 0:1], func)

            def gelus(c):
                l = c.layer
                for i in range(FT // 2):
                    if i == 0:
                        wait(act, w2_ps, c.mlp(1, 0))
                    wait(act, w1_ps, c.mlp(4, i + 1))
                    src = split3(dense[(i + 1) % 2][:])
                    for k in range(2):
                        ins = nc.scalar.activation(hid[:, 2 * i + k], src[:, k], ACT.Gelu, bias=col(l, "b1", 2 * i + k))
                    ins.then_inc(gelu_sb, 1)

            def exps(g, *pairs):
                l = g.layer
                for p in pairs:
                    if p % 2 == 0:
                        wait(act, o_ps, g.count(4, p // 2 - 1) if p >= 4 else g.count(4, p // 2 + 3 - 4))
                    for kt in range(T):
                        wait(act, st_ps, g.count(16, 2 * p + kt + 1))
                        q0 = P if CAUSAL[l] and kt else 0
                        src = split3(st_bank[kt][:])[:, :, q0:N]
                        nc.scalar.activation(probs[p % 4][:, kt, :, q0:N], src, ACT.Exp,
                                             scale=SCORE_SCALE[l]).then_inc(p_sb, 1)

            def step(g):
                c, a = g.back(1), g.ahead(1)
                inputs, mlp = inputs_of(a), c.exists and HAS_MLP[c.layer]
                if inputs:
                    modulate1(a)
                if mlp:
                    exps(g, 0)
                    if inputs:
                        query_hi(a)
                    exps(g, 1)
                    if inputs:
                        key_hi(a)
                else:
                    max_rows(act, g, 0)
                    if inputs:
                        query_hi(a)
                        key_hi(a)
                    exps(g, 0, 1)
                exps(g, 2, 3)
                if mlp:
                    modulate2(c)
                if inputs:
                    value_copy(a)
                if mlp:
                    bring_table(ACT.Gelu)
                    gelus(c)
                    bring_table(ACT.Exp)
                else:
                    max_rows(act, g, 1)
                exps(g, 4, 5, 6, 7)
                ao_transposed(g)

            act.wait_ge(consts, 1)
            act.wait_ge(vec_ld, 16)
            nc.scalar.activation(bv_scaled[:], vec[:, VECS[2, "bv"][0]:VECS[2, "bv"][0] + KT], ACT.Copy,
                                 scale=D ** -0.5).then_inc(silu_exp, 1)
            act.wait_ge(silu_exp, 2)
            for first in (Step(0), Step(1)):
                modulate1(first)
                query_hi(first)
                key_hi(first)
                value_copy(first)
            run_steps(act, step)
            modulate2(Step(STEPS - 1))
            gelus(Step(STEPS - 1))

        @block.vector
        def _(dve):
            def fill_stack(i):
                nc.vector.memset(k_stack[i][:], 1.0).then_inc(kv_filled, 1)
                nc.vector.memset(v_aug[i][:], 1.0).then_inc(kv_filled, 1)

            fill_stack(0)

            dve.wait_ge(silu_exp, 1)
            nc.vector.tensor_scalar(silu_t[:], silu_t[:], 1.0, None, ALU.add).then_inc(silu_chain, 1)
            dve.wait_ge(silu_chain, 1)
            nc.vector.reciprocal(silu_t[:], silu_t[:]).then_inc(silu_chain, 1)
            dve.wait_ge(silu_chain, 2)
            nc.vector.tensor_tensor(silu_sb[:], cond_sb[:], silu_t[:], ALU.mult).then_inc(silu_done, 1)

            chained = [0]

            def link(ins):
                chained[0] += 1
                ins.then_inc(mod_chain, 1)
                dve.wait_ge(mod_chain, chained[0])

            def modulation_cols(l, norms=(0, 1)):
                dve.wait_ge(vec_ld, 16)
                dve.wait_ge(mod_ps, 3 * l + 1 + norms[-1])
                cols = cols_bank(l, norms[0])[:, 0:64].rearrange("p (c b) -> p c b", b=B)
                tt, stt = nc.vector.tensor_tensor, nc.vector.scalar_tensor_tensor
                n0, n1 = norms[0], norms[-1] + 1
                if l == 2:
                    def vec_of(name):
                        c = VECS[l, name][0]
                        return vec[:, c:c + KT].unsqueeze(2).to_broadcast([P, KT, B])

                    fac, add = mod[:, l, 0, 0], mod[:, l, 0, 1]
                    tt(mod_t[:, 0], cols[:, 0:KT], vec_of("bg"), ALU.add)
                    link(tt(mod_t[:, 1], cols[:, KT:2 * KT], vec_of("bb"), ALU.add))
                    tt(fac, mod_t[:, 0], vec_of("lg"), ALU.mult)
                    link(tt(add, mod_t[:, 0], vec_of("lb"), ALU.mult))
                    ins = tt(add, add, mod_t[:, 1], ALU.add)
                else:
                    def vec_of(name, per_norm, i):
                        c = VECS[l, name][0]
                        v = vec[:, c:c + 2 * per_norm * KT].rearrange("p (n s t) -> p n s t", n=2, s=per_norm)
                        return v[:, n0:n1, i].unsqueeze(3).to_broadcast([P, n1 - n0, KT, B])

                    shift, scale = (cols.rearrange("p (n s t) b -> p n s t b", n=2, s=2)[:, n0:n1, i] for i in range(2))
                    fac, add = (mod[:, l, n0:n1, i] for i in range(2))

                    def scale_plus_one():
                        for n in range(n1 - n0):
                            ins = stt(fac[:, n], scale[:, n], 1.0, vec_of("ada", 3, 1)[:, n], ALU.add, ALU.add)
                        return ins

                    if l == 0:
                        scale_plus_one()
                        ins = tt(add, shift, vec_of("ada", 3, 0), ALU.add)
                    else:
                        tt(mod_t[:, n0:n1], shift, vec_of("ada", 3, 0), ALU.add)
                        link(scale_plus_one())
                        link(tt(add, fac, vec_of("g1", 2, 1), ALU.mult))
                        tt(fac, fac, vec_of("g1", 2, 0), ALU.mult)
                        ins = tt(add, add, mod_t[:, n0:n1], ALU.add)
                ins.then_inc(mod_cols, len(norms))
                dve.wait_ge(mod_cols, 2 * l + 1 + norms[-1])

            def modulation_rows(l):
                dve.wait_ge(row_ld, 16 * (l + 1))
                if l > 0:
                    dve.wait_ge(par_st, 16 * l)
                if l > 1:
                    dve.wait_ge(x2_done, MOD_STEP[l - 1])
                dve.wait_ge(mod_ps, 3 * l + 3)
                r = dense[0][0:B, :].rearrange("p (a d) -> p a d", a=2)
                if l == 2:
                    link(nc.vector.tensor_tensor(row_t[:, 0], r[:, 0], row_in[:, 0], ALU.add))
                    nc.vector.tensor_tensor(row_out[:, 2], row_t[:, 0], row_in[:, 1], ALU.mult)
                    nc.vector.tensor_copy(row_out[:, 0], row_in[:, 4])
                    nc.vector.tensor_copy(row_out[:, 1], row_in[:, 4])
                    link(nc.vector.tensor_tensor(row_t[:, 1], r[:, 1], row_in[:, 2], ALU.add))
                    link(nc.vector.tensor_tensor(row_t[:, 0], row_t[:, 0], row_in[:, 3], ALU.mult))
                    nc.vector.tensor_tensor(row_out[:, 3], row_t[:, 0], row_t[:, 1], ALU.add).then_inc(mod_done, 1)
                else:
                    link(nc.vector.tensor_tensor(row_out[:, 0], r[:, 0], row_in[:, 0], ALU.add))
                    link(nc.vector.tensor_tensor(row_out[:, 2], r[:, 1], row_in[:, 2], ALU.add))
                    nc.vector.tensor_tensor(row_out[:, 1], row_out[:, 0], row_in[:, 1], ALU.mult)
                    nc.vector.tensor_tensor(row_out[:, 3], row_out[:, 2], row_in[:, 3], ALU.mult).then_inc(mod_done, 1)
                dve.wait_ge(mod_done, l + 1)

            def x_of(i):
                return x_sb[:, bass.ds(i.wrapped_seq, 1)][:, 0] if i.reg is not None else x_sb[:, i.seq]

            def norm_stats(src, which, s):
                for t in range(T):
                    ins = nc.vector.bn_stats(stats[:, which, t], src[:, t])
                ins.then_inc(s, 1)

            def norm_mv(which, s):
                for t in range(T):
                    ins = nc.vector.bn_aggr(mv[:, which, t], stats[:, which, t])
                ins.then_inc(s, 1)

            def normalize(i, src, which, rstd_s, dst, s):
                wait(dve, rstd_s, i.count(1, 1))
                for t in range(T):
                    ins = nc.vector.tensor_scalar(dst[:, t], src[:, t], mv[:, which, t, 0:1], rstd[:, which, t:t + 1],
                                                  ALU.subtract, ALU.mult)
                ins.then_inc(s, 1)

            def ln1_a(i):
                if i.layer == 0:
                    for q in range(3):
                        if q <= min(i.off, 2):
                            dve.wait_ge(x_ld[q], 32 if q == 2 else 16)
                norm_stats(x_of(i), 0, ln1_stats)

            def ln1_c(i):
                wait(dve, ht1_ps, i.count(1, 0))
                normalize(i, x_of(i), 0, ln1_rstd, xn1, xn1_done)

            def score_max(g, j):
                p, qt = j // 2, j % 2
                wait(dve, s_ps, g.count(16, j + 1))
                bank = s_bank[(j + (j >= 8)) % 2]
                k1 = P if CAUSAL[g.layer] and qt == 0 else N
                nc.vector.tensor_reduce(neg_max[:, qt, 2 * p:2 * p + 2], split3(bank[:])[:, :, 0:k1], AX.X, ALU.max,
                                        negate=True).then_inc(s_max, 1)

            def max_split(g, half):
                h0 = half * H // 2
                hi = max_parts[:, half, :, 0]
                lo = max_parts[:, half, :, 1]
                src = neg_max[:, :, h0:h0 + H // 2]
                wait(dve, max_ps, g.count(2, half + 1 - 2))
                wait(dve, s_max, g.count(16, 8 * half + 8))
                nc.vector.tensor_copy(hi.bitcast(F32R), src).then_inc(max_hi, 1)
                wait(dve, max_hi, g.count(2, half + 1))
                nc.vector.tensor_tensor(lo.bitcast(F32R), src, hi, ALU.subtract).then_inc(max_lo, 1)

            def max_copy(g, half):
                wait(dve, max_ps, g.count(2, half + 1))
                wait(dve, max_ld, g.count(64, 32 * half + 32 - 64))
                nc.vector.tensor_copy(max_t[half][:], s_bank[half % 2][0:H, 0:N]).then_inc(max_sb, 1)

            def lo_part(a, which, bank, ready, hi, dst, s, spilled):
                l = a.layer
                wait(dve, spilled, a.count(32, 0))
                wait(dve, ready, a.count(1, 1))
                src = split3(dense[bank][:])
                if QKV_BIAS[l]:
                    for t in range(KT):
                        ins = nc.vector.scalar_tensor_tensor(dst[:, t].bitcast(F32R), src[:, t], col(l, which, t), hi[:, t],
                                                             ALU.add, ALU.subtract)
                else:
                    ins = nc.vector.tensor_tensor(dst[:].bitcast(F32R), src, hi[:], ALU.subtract)
                ins.then_inc(s, 1)

            def times_gate(c, src, row, s):
                for t in range(T):
                    ins = nc.vector.tensor_tensor(prod[:, t], src[:, t], par_sb[c.par][:, row], ALU.mult)
                ins.then_inc(s, 1)

            def residual(c, dst, src, which, ready, s):
                wait(dve, ready, c.count(1, 1))
                nc.vector.tensor_tensor(dst, src, xg[which][:], ALU.add).then_inc(s, 1)

            def first_residual(c):
                wait(dve, proj_ps, c.count(1, 1))
                wait(dve, par_ld, c.count(16, 16))
                wait(dve, x2_done, c.count(1, 0))
                if c.layer == 2:
                    residual(c, x1[:], split3(o_bank[0][:]), 0, xg1, x1_done)
                else:
                    times_gate(c, split3(o_bank[0][:]), 0, prod1)
                    wait(dve, prod1, c.mlp(1, 1))
                    residual(c, x1[:], prod[:], 0, xg1, x1_done)

            def second_residual(c):
                if c.layer == 2:
                    wait(dve, xn2_done, c.count(1, 1))
                    times_gate(c, xn2, 2, prod2)
                else:
                    wait(dve, w2_ps, c.mlp(1, 1))
                    times_gate(c, split3(dense[1][:]), 2, prod2)
                wait(dve, prod2, c.count(1, 1))
                residual(c, x_of(c), prod[:], 1, xg2, x2_done)

            def out_copy(g, q):
                wait(dve, o_ps, g.count(4, q + 1))
                wait(dve, ot_ps, g.count(4, q + 1 - 2))
                nc.vector.tensor_copy(o_sb[q % 2][:], o_bank[q % 2][:, 0:N]).then_inc(o_copy, 1)

            def out_norm(g, q):
                wait(dve, ot_ps, g.count(4, q + 1))
                o4 = o_bank[q % 2][:, N:2 * N].rearrange("p (t h d) -> p t h d", t=T, h=4)
                wait(dve, ao_sb, g.count(4, q))
                nc.vector.reciprocal(rec[:], o4[:, :, :, HD]).then_inc(rec_sb, 1)
                wait(dve, rec_sb, g.count(4, q + 1))
                if q == 0:
                    wait(dve, aot_ps, g.count(1, 0))
                dst = ao[:, :, 4 * HD * q:4 * HD * (q + 1)].rearrange("p t (h d) -> p t h d", h=4)
                nc.vector.tensor_tensor(dst, o4[:, :, :, 0:HD],
                                        rec[:].unsqueeze(3).to_broadcast([P, T, 4, HD]), ALU.mult).then_inc(ao_sb, 1)

            def second_norm(c):
                if c.layer != 2:
                    wait(dve, w1_ps, c.mlp(4, 0))
                normalize(c, x1, 1, ln2_rstd, xn2, xn2_done)

            def ht2_split(c):
                wait(dve, ht2_raw_sb, c.mlp(1, 1))
                nc.vector.tensor_copy(ht2[:].bitcast(F32R), ht2_raw[:]).then_inc(ht2_hi_sb, 1)
                wait(dve, ht2_hi_sb, c.mlp(1, 1))
                nc.vector.tensor_tensor(ht2_lo[:].bitcast(F32R), ht2_raw[:], ht2[:], ALU.subtract).then_inc(ht2_sb, 1)

            def query_lo(a):
                lo_part(a, "bq", 0, q_hi_sb, q_hi, q_lo, q_lo_sb, q_spill)

            def key_lo(a):
                lo_part(a, "bk", 1, k_hi_sb, k_hi, k_lo, k_lo_sb, k_spill)

            def maxima(g, *tiles):
                for j in tiles:
                    score_max(g, j)

            def step(g):
                c, a, n = g.back(1), g.ahead(1), g.ahead(2)
                inputs = inputs_of(a)
                modulated = modulation_of(g)
                maxima(g, 8, 9)
                if c.exists and HAS_MLP[c.layer]:
                    first_residual(c)
                    wait(dve, x1_done, c.count(1, 1))
                    norm_stats(x1, 1, ln2_stats)
                    wait(dve, ln2_stats, c.count(1, 1))
                    maxima(g, 10)
                    norm_mv(1, ln2_mv)
                    if inputs:
                        query_lo(a)
                    second_norm(c)
                    if inputs:
                        key_lo(a)
                    maxima(g, 11)
                    out_copy(g, 0)
                    maxima(g, 12)
                    ht2_split(c)
                    maxima(g, 13)
                    out_norm(g, 0)
                    out_copy(g, 1)
                    maxima(g, 14)
                    out_norm(g, 1)
                    maxima(g, 15)
                    max_split(g, 1)
                    max_copy(g, 1)
                    if n.exists:
                        ln1_a(n)
                        wait(dve, ln1_stats, n.count(1, 1))
                else:
                    if inputs:
                        query_lo(a)
                        key_lo(a)
                    maxima(g, 10, 11, 12, 13, 14, 15)
                    max_split(g, 1)
                    max_copy(g, 1)
                    if c.exists:
                        first_residual(c)
                        wait(dve, x1_done, c.count(1, 1))
                        norm_stats(x1, 1, ln2_stats)
                        wait(dve, ln2_stats, c.count(1, 1))
                    out_copy(g, 0)
                    if c.exists:
                        norm_mv(1, ln2_mv)
                    out_norm(g, 0)
                    out_copy(g, 1)
                    if c.exists:
                        second_norm(c)
                    out_norm(g, 1)
                if c.exists and HAS_MLP[c.layer]:
                    if a.exists:
                        maxima(a, 0)
                    if n.exists:
                        norm_mv(0, ln1_mv)
                    if a.exists:
                        maxima(a, 1)
                    if n.exists:
                        ln1_c(n)
                    if a.exists:
                        maxima(a, 2)
                    out_copy(g, 2)
                    out_norm(g, 2)
                    if a.exists:
                        maxima(a, 3)
                    out_copy(g, 3)
                    if a.exists:
                        maxima(a, 4)
                    out_norm(g, 3)
                    if modulated:
                        modulation_cols(modulated)
                    if a.exists:
                        maxima(a, 5, 6, 7)
                        max_split(a, 0)
                        max_copy(a, 0)
                    second_residual(c)
                    if modulated:
                        modulation_rows(modulated)
                else:
                    maxima(a, 0, 1, 2)
                    if n.exists:
                        ln1_a(n)
                        wait(dve, ln1_stats, n.count(1, 1))
                    maxima(a, 3)
                    if n.exists:
                        norm_mv(0, ln1_mv)
                    out_copy(g, 2)
                    maxima(a, 4)
                    out_norm(g, 2)
                    if n.exists:
                        ln1_c(n)
                    maxima(a, 5)
                    out_copy(g, 3)
                    maxima(a, 6)
                    out_norm(g, 3)
                    if modulated:
                        modulation_cols(modulated)
                    maxima(a, 7)
                    max_split(a, 0)
                    max_copy(a, 0)
                    if c.exists:
                        second_residual(c)
                    if modulated:
                        modulation_rows(modulated)

            def first_norm(i):
                ln1_a(i)
                dve.wait_ge(ln1_stats, i.off + 1)
                norm_mv(0, ln1_mv)
                ln1_c(i)

            first_norm(Step(0))
            modulation_cols(0, (0,))
            fill_stack(1)
            modulation_cols(0, (1,))
            first_norm(Step(1))
            query_lo(Step(0))
            key_lo(Step(0))
            modulation_rows(0)
            query_lo(Step(1))
            key_lo(Step(1))
            maxima(Step(0), *range(8))
            max_split(Step(0), 0)
            max_copy(Step(0), 0)
            run_steps(dve, step)
            last = Step(STEPS - 1)
            first_residual(last)
            wait(dve, x1_done, last.count(1, 1))
            norm_stats(x1, 1, ln2_stats)
            dve.wait_ge(ln2_stats, last.count(1, 1))
            norm_mv(1, ln2_mv)
            wait(dve, w1_ps, last.mlp(4, 0))
            normalize(last, x1, 1, ln2_rstd, xn2, xn2_done)
            ht2_split(last)
            second_residual(last)

        @block.tensor
        def _(pe):
            mm, tr = nc.tensor.matmul, nc.tensor.transpose

            def modulation_cols(l, norms=(0, 1)):
                if l == 0 and norms == (0,):
                    pe.wait_ge(ada_first_ld, 16)
                else:
                    pe.wait_ge(ada_ld, 16 * (l + 1))
                pe.wait_ge(cond_ld, 16)
                if l in (1, 3):
                    pe.wait_ge(silu_done, 1)
                cs = silu_sb if l in (1, 3) else cond_sb
                for norm in (0,) if l == 2 else norms:
                    for i in range(2 * KT):
                        ch, to = norm * 3 * KT + i, (norm * 2 * KT + i) * B
                        for kt in range(KT):
                            ins = mm(cols_bank(l, norm)[:, to:to + B], ada_cols(l, kt, ch * P, (ch + 1) * P), cs[:, kt],
                                     start=kt == 0, stop=kt == KT - 1)
                ins.then_inc(mod_ps, len(norms))

            def modulation_rows(l):
                pe.wait_ge(mod_cols, 2 * (l + 1))
                cs = silu_sb if l in (1, 3) else cond_sb
                for i, ch in enumerate((0, 1) if l == 2 else (2, 5)):
                    for kt in range(KT):
                        ins = mm(dense[0][0:B, i * D:(i + 1) * D], cs[:, kt], ada_cols(l, kt, ch * D, (ch + 1) * D),
                                 start=kt == 0, stop=kt == KT - 1)
                ins.then_inc(mod_ps, 1)

            def ada_cols(l, kt, c0, c1):
                return ada_sb[:, kt, c0:c1]

            def transposed(bank, src, ready):
                for t in range(T):
                    for kt in range(KT):
                        ins = tr(bank[:, kt * N + t * P:kt * N + (t + 1) * P], src[:, t, kt * P:(kt + 1) * P], ident[:])
                ins.then_inc(ready, 1)

            def ht1_t(a):
                wait(pe, xn1_done, a.count(1, 1))
                wait(pe, v_sb, a.count(1, 0))
                wait(pe, ao_sb, a.count(4, 4 - 2 * 4))
                transposed(o_bank[1], xn1, ht1_ps)

            def q_product(a, t):
                if t == 0:
                    pe.wait_ge(wqkv_ld[a.layer], 16)
                    wait(pe, ht1_sb, a.count(1, 1))
                    wait(pe, q_lo_sb, a.count(1, 0))
                    if a.off > 1:
                        pe.wait_ge(mod_done, modulations_before(a.back(1)))
                qk_product(a, 0, t, 0, q_ps)

            def qk_product(a, which, t, bank, ready):
                for kt in range(KT):
                    c0 = which * D + t * P
                    ins = mm(dense[bank][:, t * N:(t + 1) * N], w_qkv(a.layer, kt, c0, c0 + P), ht1[:, kt],
                             start=kt == 0, stop=kt == KT - 1)
                if t == KT - 1:
                    ins.then_inc(ready, 1)

            def k_product(a):
                wait(pe, k_lo_sb, a.count(1, 0))
                c = a.back(2)
                if c.off > 0 or c.reg is not None:
                    wait(pe, prod2, c.count(1, 0))
                for t in range(KT):
                    qk_product(a, 1, t, 1, k_ps)

            def v_product(a, t):
                for kt in range(KT):
                    ins = mm(o_bank[1][:, t * D:(t + 1) * D], ht1[:, kt, t * P:(t + 1) * P],
                             w_qkv(a.layer, kt, 2 * D, 3 * D), start=kt == 0, stop=kt == KT - 1)
                if t == T - 1:
                    ins.then_inc(v_ps, 1)

            def ao_turn(g):
                wait(pe, ao_sb, g.count(4, 4))
                transposed(o_bank[0], ao, aot_ps)

            def projection(c, t):
                if t == 0:
                    pe.wait_ge(w_ld[c.layer], 16)
                    wait(pe, aot_sb, c.count(1, 1))
                for kt in range(KT):
                    ins = mm(o_bank[0][:, t * D:(t + 1) * D], ao_t[:, kt, t * P:(t + 1) * P], w_o(c.layer, kt),
                             start=kt == 0, stop=kt == KT - 1)
                if t == T - 1:
                    ins.then_inc(proj_ps, 1)

            def ht2_t(c, a):
                wait(pe, xn2_done, c.count(1, 1))
                if a is not None and a.exists:
                    wait(pe, q_lo_sb, a.count(1, 1))
                transposed(dense[0], xn2, ht2_ps)

            def mlp_up(c, a, i, k):
                if k == 0:
                    if i == 0:
                        wait(pe, ht2_sb, c.mlp(1, 1))
                        if a is not None and a.exists:
                            wait(pe, k_lo_sb, a.count(1, 1))
                    elif i > 1:
                        wait(pe, gelu_sb, c.mlp(4, i - 1))
                    pe.wait_ge(w1_split, (c.layer - (c.layer > 2)) * FT // 2 + i + 1)
                j = 2 * i + k
                terms = [(w_1(c.layer, w, kt, j), h[:, kt]) for kt in range(KT)
                         for w, h in ((w1_hi, ht2), (w1_hi, ht2_lo), (w1_lo, ht2))]
                for n, (w, h) in enumerate(terms):
                    ins = mm(dense[(i + 1) % 2][:, k * N:(k + 1) * N], w, h.bitcast(F32R),
                             start=n == 0, stop=n == len(terms) - 1)
                if k == 1:
                    ins.then_inc(w1_ps, 1)

            def mlp_down(c, lo, hi):
                for i in range(lo, hi):
                    t, j = i // FT, i % FT
                    if i == 0:
                        pe.wait_ge(w2_ld[c.layer], 16)
                        wait(pe, gelu_sb, c.mlp(4, 3))
                    if i == 6:
                        wait(pe, gelu_sb, c.mlp(4, 4))
                    ins = mm(dense[1][:, t * D:(t + 1) * D], hid[:, j, t * P:(t + 1) * P], w_2(c.layer, j),
                             start=j == 0, stop=j == FT - 1)
                    if i == T * FT - 1:
                        ins.then_inc(w2_ps, 1)

            def score(g, *tiles):
                for j in tiles:
                    p, qt = j // 2, j % 2
                    pos = j + (j >= 8)
                    if j == 0:
                        wait(pe, stack_ld, g.count(144, 144))
                        wait(pe, s_max, g.count(16, 0))
                    elif j == 1:
                        wait(pe, max_sb, g.count(2, 0))
                    elif j == 9:
                        wait(pe, max_sb, g.count(2, 1))
                    elif j == 8:
                        wait(pe, s_max, g.count(16, 8))
                    else:
                        wait(pe, s_max, g.count(16, j - 1))
                    bank = s_bank[pos % 2]
                    causal = CAUSAL[g.layer]
                    k1 = P if causal and qt == 0 else N
                    for e in range(2):
                        ins = mm(bank[:, e * N:e * N + k1],
                                 q_stack[g.par][0:KB, 2 * p + e, qt * P:(qt + 1) * P].bitcast(F32R),
                                 k_stack[g.par][0:KB, p, 0:k1].bitcast(F32R), start=True, stop=not causal)
                        if causal:
                            ins = mm(bank[:, e * N + k1 - P:e * N + k1], ident_b[:], mask_q[:, 0], start=False, stop=True)
                    ins.then_inc(s_ps, 1)

            def max_turn(g, half):
                wait(pe, max_lo, g.count(2, half + 1))
                wait(pe, s_max, g.count(16, 7 if half == 0 else 16))
                for qt in range(T):
                    ins = tr(s_bank[half % 2][0:H, qt * P:(qt + 1) * P],
                             max_parts[:, half, qt].rearrange("p a h -> p (a h)"), ident[:])
                ins.then_inc(max_ps, 1)

            def score_t(g, *pairs):
                for p in pairs:
                    if p == 0:
                        wait(pe, max_ld, g.count(64, 32))
                    if p == PAIRS // 2:
                        wait(pe, max_ld, g.count(64, 64))
                    for kt in range(T):
                        wait(pe, p_sb, g.count(16, 2 * p + kt - 1))
                        causal = CAUSAL[g.layer]
                        q0 = P if causal and kt else 0
                        bank = split3(st_bank[kt][:])
                        ins = mm(bank[:, :, q0:N], k_stack[g.par][0:KM, p, kt * P:(kt + 1) * P].bitcast(F32R),
                                 q_stack[g.par][0:KM, 2 * p:2 * p + 2, q0:N].bitcast(F32R), start=True, stop=not causal)
                        if causal:
                            ins = mm(bank[:, :, kt * P:(kt + 1) * P], ident_b[:], mask_k[:], start=False, stop=True)
                        ins.then_inc(st_ps, 1)

            def values(g, q):
                if q == 0:
                    wait(pe, v_sb, g.count(1, 1))
                if q == 0 and g.off > 0:
                    wait(pe, x1_done, g.count(1, 0))
                elif q == 1:
                    if g.ahead(1).exists:
                        wait(pe, v_sb, g.count(1, 2))
                elif q > 1:
                    wait(pe, ao_sb, g.count(4, q - 1))
                wait(pe, p_sb, g.count(16, 4 * q + 4))
                for kt in range(T):
                    q0 = P if CAUSAL[g.layer] and kt else 0
                    for j in range(4):
                        pr = probs[(2 * q + j // 2) % 4]
                        ins = mm(o_bank[q % 2][32 * j:32 * j + 32, q0:N], v_aug[g.par][:, kt, 4 * q + j, :],
                                 pr[:, kt, j % 2, q0:N], start=kt == 0, stop=kt == T - 1)
                ins.then_inc(o_ps, 1)

            def out_turn(g, q):
                wait(pe, o_copy, g.count(4, q + 1))
                for t in range(T):
                    ins = tr(o_bank[q % 2][:, N + t * P:N + (t + 1) * P], o_sb[q % 2][:, t * P:(t + 1) * P], ident[:])
                ins.then_inc(ot_ps, 1)

            def step(g):
                c, a, n = g.back(1), g.ahead(1), g.ahead(2)
                inputs = inputs_of(a)
                modulated = modulation_of(g)
                score(g, 8, 9)
                if c.exists and HAS_MLP[c.layer]:
                    projection(c, 0)
                    projection(c, 1)
                    score(g, 10)
                    if inputs:
                        q_product(a, 0)
                    score_t(g, 0)
                    if inputs:
                        q_product(a, 1)
                    score_t(g, 1)
                    if inputs:
                        k_product(a)
                    score(g, 11)
                    score_t(g, 2)
                    values(g, 0)
                    score(g, 12)
                    if inputs:
                        v_product(a, 0)
                    score_t(g, 3)
                    ht2_t(c, a)
                    if inputs:
                        v_product(a, 1)
                    out_turn(g, 0)
                    score(g, 13)
                    values(g, 1)
                    mlp_up(c, a, 0, 0)
                    score(g, 14)
                    out_turn(g, 1)
                    mlp_up(c, a, 0, 1)
                    score(g, 15)
                    mlp_up(c, a, 1, 0)
                    mlp_up(c, a, 1, 1)
                    max_turn(g, 1)
                    mlp_up(c, a, 2, 0)
                    mlp_up(c, a, 2, 1)
                    mlp_up(c, a, 3, 0)
                    mlp_up(c, a, 3, 1)
                    if a.exists:
                        score(a, 0)
                    mlp_down(c, 0, 2)
                    score_t(g, 4)
                    if a.exists:
                        score(a, 1)
                    mlp_down(c, 2, 5)
                    score_t(g, 5)
                    if a.exists:
                        score(a, 2)
                    mlp_down(c, 5, 7)
                    values(g, 2)
                    score_t(g, 6)
                    if a.exists:
                        score(a, 3)
                    mlp_down(c, 7, 8)
                    out_turn(g, 2)
                    score_t(g, 7)
                    if a.exists:
                        score(a, 4)
                    mlp_down(c, 8, 10)
                    if modulated:
                        modulation_cols(modulated)
                    values(g, 3)
                    if a.exists:
                        score(a, 5)
                    mlp_down(c, 10, 11)
                    out_turn(g, 3)
                    mlp_down(c, 11, 12)
                    if a.exists:
                        score(a, 6)
                    ao_turn(g)
                    if a.exists:
                        score(a, 7)
                    mlp_down(c, 12, 15)
                    if a.exists:
                        max_turn(a, 0)
                    mlp_down(c, 15, 16)
                    if modulated:
                        modulation_rows(modulated)
                    if n.exists:
                        ht1_t(n)
                else:
                    if inputs:
                        q_product(a, 0)
                        q_product(a, 1)
                        k_product(a)
                    score_t(g, 0)
                    score(g, 10, 11)
                    if inputs:
                        v_product(a, 0)
                    score_t(g, 1)
                    score(g, 12, 13)
                    if inputs:
                        v_product(a, 1)
                    score(g, 14, 15)
                    score_t(g, 2)
                    if c.exists:
                        projection(c, 0)
                    max_turn(g, 1)
                    score_t(g, 3)
                    if c.exists:
                        projection(c, 1)
                    values(g, 0)
                    out_turn(g, 0)
                    values(g, 1)
                    score_t(g, 4)
                    out_turn(g, 1)
                    score(a, 0, 1)
                    score_t(g, 5)
                    score(a, 2, 3)
                    score_t(g, 6)
                    values(g, 2)
                    score(a, 4)
                    score_t(g, 7)
                    out_turn(g, 2)
                    score(a, 5)
                    if modulated:
                        wait(pe, q_lo_sb, a.count(1, 1))
                        modulation_cols(modulated)
                    values(g, 3)
                    score(a, 6)
                    out_turn(g, 3)
                    score(a, 7)
                    ao_turn(g)
                    if n.exists:
                        ht1_t(n)
                    max_turn(a, 0)
                    if modulated:
                        modulation_rows(modulated)

            def products(a):
                q_product(a, 0)
                q_product(a, 1)
                k_product(a)
                for t in range(T):
                    v_product(a, t)

            pe.wait_ge(consts, 6)
            first = Step(0)
            ht1_t(first)
            modulation_cols(0, (0,))
            modulation_cols(0, (1,))
            products(first)
            pe.wait_ge(q_lo_sb, 1)
            modulation_rows(0)
            ht1_t(Step(1))
            pe.wait_ge(mod_done, 1)
            products(Step(1))
            score(first, *range(8))
            max_turn(first, 0)
            run_steps(pe, step)
            last = Step(STEPS - 1)
            for t in range(T):
                projection(last, t)
            ht2_t(last, None)
            for i in range(FT // 2):
                for k in range(2):
                    mlp_up(last, None, i, k)
            mlp_down(last, 0, T * FT)


def _pack(inputs):
    g = {k: np.asarray(v) for k, v in inputs.items()}

    def tiles(w):
        return w.reshape(-1, P, w.shape[1]).transpose(1, 0, 2)

    def L(l, name):
        return g[f"L{l}_cond_{name}"]

    qkv2 = L(2, "Wqkv").reshape(D, 3, D).transpose(2, 1, 0).reshape(D, 3 * D)
    bqkv2 = L(2, "bqkv").reshape(D, 3).T
    weights = [
        (np.concatenate([L(0, "Wq"), L(0, "Wk"), L(0, "Wv")], 1), L(0, "Wo"), L(0, "W1"), L(0, "W2")),
        (L(1, "Wqkv"), L(1, "Wproj"), L(1, "W1"), L(1, "W2")),
        (qkv2, L(2, "Wp").T),
        (L(3, "Wqkv"), L(3, "Wproj"), L(3, "W1"), L(3, "W2")),
    ]
    ada = [L(0, "W_ada"), L(1, "Wada"), np.concatenate([L(2, "Wg").T, L(2, "Wb").T], 1), L(3, "Wt")]
    biases = (L(0, "b_ada"), L(1, "bada"), None, L(3, "bt"))
    vec = {
        (0, "ada"): biases[0], (0, "bq"): L(0, "bq"), (0, "bk"): L(0, "bk"), (0, "bv"): L(0, "bv"), (0, "b1"): L(0, "b1"),
        (1, "ada"): biases[1], (1, "b1"): L(1, "b1"),
        (2, "lg"): L(2, "ln_g"), (2, "lb"): L(2, "ln_b"), (2, "bg"): L(2, "bg"), (2, "bb"): L(2, "bb"),
        (2, "bq"): bqkv2[0], (2, "bk"): bqkv2[1], (2, "bv"): bqkv2[2],
        (3, "ada"): biases[3], (3, "bq"): L(3, "bqkv")[0:D], (3, "bk"): L(3, "bqkv")[D:2 * D],
        (3, "bv"): L(3, "bqkv")[2 * D:], (3, "b1"): L(3, "b1"),
    }
    for l in (1, 3):
        for n in ("g1", "be1", "g2", "be2"):
            vec[l, n] = L(l, n)
    vecs = np.concatenate([vec[k].reshape(-1, P) for k in VECS], 0).T
    rows = []
    for l in range(LAYERS):
        if l == 2:
            r = [L(2, "bg"), L(2, "ln_g"), L(2, "bb"), L(2, "ln_b"), L(2, "bp")]
        else:
            bo, b2 = L(l, "bo" if l == 0 else "bproj"), L(l, "b2")
            r = [biases[l][2 * D:3 * D], bo, biases[l][5 * D:], b2, b2]
        rows.append(np.stack(r))
    packed = {"x": g["x"], "cond_t": g["cond_1024"].T.reshape(KT, P, B).transpose(1, 0, 2), "vecs": vecs,
              "rows": np.stack(rows)}
    for l in range(LAYERS):
        packed[f"ada{l}"] = tiles(ada[l])
        packed[f"w{l}"] = np.concatenate([tiles(w).reshape(P, -1) for w in weights[l]], 1)
    return {k: np.ascontiguousarray(v) for k, v in packed.items()}


def kernel(**inputs):
    import concourse.bacc as _bacc
    from concourse.bass_utils import run_bass_kernel_spmd as _run

    nc = _bacc.Bacc("TRN2", target_bir_lowering=False, num_devices=1)
    arrays = _pack(inputs)
    t = {k: nc.dram_tensor(k, a.shape, mybir.dt.from_np(a.dtype), kind="ExternalInput").ap() for k, a in arrays.items()}
    out = nc.dram_tensor("out", (B, N, D), F32, kind="ExternalOutput").ap()
    cond_seq_blocks(nc, t["x"], t["cond_t"], t["vecs"], t["rows"], [t[f"ada{l}"] for l in range(LAYERS)],
                    [t[f"w{l}"] for l in range(LAYERS)], out)
    return _run(nc, [arrays], core_ids=[0]).results[0]["out"]
```
